# Optimizing a Trainium2 kernel written in Bass

```python
import numpy as np
import jax
import jax.numpy as jnp

def _softmax(x, axis=-1):
    return jax.nn.softmax(x, axis=axis)

def _gelu(x):
    return jax.nn.gelu(x, approximate=True)

def _silu(x):
    return jax.nn.silu(x)

def _sigmoid(x):
    return jax.nn.sigmoid(x)

def _layernorm(x, axis=-1, eps=1e-05):
    m = jnp.mean(x, axis=axis, keepdims=True)
    v = jnp.var(x, axis=axis, keepdims=True)
    return (x - m) / jnp.sqrt(v + eps)

def _scatter_add(tgt, idx, src, axis=0):
    return tgt.at[idx].add(src)

def _segment_sum(src, seg, n):
    return jax.ops.segment_sum(src, seg, n)
kernel_name = 'mk_flamingo_gated_d1_seqx_r8_9b2ece'

def setup_inputs(seed: int=0):
    np.random.seed(seed)
    _w = jnp.asarray

    def _rec_inputs():
        import jax
        import jax.numpy as jnp
        _rk = jax.random.key(seed)
        x = -0.0003929 + 0.9999 * jax.random.normal(jax.random.fold_in(_rk, 1), (2, 512, 128), jnp.float32)
        _lenS = 512 - jax.random.randint(jax.random.fold_in(_rk, 7), (2,), 0, max(1, 512 // 4) + 1, jnp.int32)
        _lenS2 = 77 - jax.random.randint(jax.random.fold_in(_rk, 8), (2,), 0, max(1, 77 // 4) + 1, jnp.int32)
        _ctx_1024P = jax.random.normal(jax.random.fold_in(_rk, 11), (2, 16, 128), jnp.float32)
        _ctx_1024c = jax.random.dirichlet(jax.random.fold_in(_rk, 511), 0.3 * jnp.ones((16,), jnp.float32), (2, 77))
        _ctx_1024t = jnp.einsum('bsk,bkd->bsd', _ctx_1024c, _ctx_1024P)
        _ctx_1024t = _ctx_1024t * jax.lax.rsqrt(jnp.mean(jnp.square(_ctx_1024t)) + 1e-12) * 0.953939
        ctx_1024 = 2.81802e-05 + 1.00001 * (_ctx_1024t + 0.3 * jax.random.normal(jax.random.fold_in(_rk, 611), (2, 77, 128), jnp.float32))
        _g = jax.random.normal(jax.random.fold_in(_rk, 9001), (2, 1), jnp.float32)
        _g = jnp.sign(_g) * jnp.maximum(jnp.abs(_g), 1.0) + (_g == 0) * 1.0
        g_xattn = _g[0]
        g_ffn = _g[1]
        return (x, ctx_1024, g_xattn, g_ffn)
    x, ctx_1024, g_xattn, g_ffn = _rec_inputs()

    def _L0_xattn_setup():
        import jax, jax.numpy as jnp
        import numpy as np
        EMBED = 128
        B, I, J = (8, 256, 256)
        SCALE = EMBED ** (-0.5)
        key = jax.random.key(seed)
        ks = jax.random.split(key, 5)
        s = EMBED ** (-0.5)
        return {'q_in': jax.random.normal(ks[0], (B, I, EMBED), dtype=jnp.float32), 'k_v': jax.random.normal(ks[1], (B, J, EMBED), dtype=jnp.float32), 'Wq': jax.random.normal(ks[2], (EMBED, EMBED), dtype=jnp.float32) * s, 'bq': jnp.zeros((EMBED,), dtype=jnp.float32), 'Wk': jax.random.normal(ks[3], (EMBED, EMBED), dtype=jnp.float32) * s, 'bk': jnp.zeros((EMBED,), dtype=jnp.float32), 'Wv': jax.random.normal(ks[4], (EMBED, EMBED), dtype=jnp.float32) * s, 'bv': jnp.zeros((EMBED,), dtype=jnp.float32)}
    _L0_xattn_all = _L0_xattn_setup()
    _L0_xattn_in = {k: v for k, v in _L0_xattn_all.items() if k in ('Wq', 'bq', 'Wk', 'bk', 'Wv', 'bv')}
    del _L0_xattn_all

    def _L0_ffn_setup():
        import jax, jax.numpy as jnp
        import numpy as np
        TOP_K = 2
        key = jax.random.key(seed)
        k1, k2, k3, k4 = jax.random.split(key, 4)
        B, T, D, H, E = (2, 256, 128, 256, 8)
        x = jax.random.normal(k1, (B, T, D), dtype=jnp.float32)
        w12 = jax.random.normal(k2, (E, 2 * H, D), dtype=jnp.float32) * D ** (-0.5)
        w3 = jax.random.normal(k3, (E, D, H), dtype=jnp.float32) * H ** (-0.5)
        gate_w = jax.random.normal(k4, (E, D), dtype=jnp.float32) * D ** (-0.5)
        return {'x': x, 'w12': w12, 'w3': w3, 'gate_w': gate_w}
    _L0_ffn_all = _L0_ffn_setup()
    _L0_ffn_in = {k: v for k, v in _L0_ffn_all.items() if k in ('w12', 'w3', 'gate_w')}
    del _L0_ffn_all
    return {'x': x, 'ctx_1024': ctx_1024, 'g_xattn': g_xattn, 'g_ffn': g_ffn, 'L0_xattn_Wq': _L0_xattn_in['Wq'], 'L0_xattn_bq': _L0_xattn_in['bq'], 'L0_xattn_Wk': _L0_xattn_in['Wk'], 'L0_xattn_bk': _L0_xattn_in['bk'], 'L0_xattn_Wv': _L0_xattn_in['Wv'], 'L0_xattn_bv': _L0_xattn_in['bv'], 'L0_ffn_w12': _L0_ffn_in['w12'], 'L0_ffn_w3': _L0_ffn_in['w3'], 'L0_ffn_gate_w': _L0_ffn_in['gate_w']}

def reference(x, ctx_1024, g_xattn, g_ffn, L0_xattn_Wq, L0_xattn_bq, L0_xattn_Wk, L0_xattn_bk, L0_xattn_Wv, L0_xattn_bv, L0_ffn_w12, L0_ffn_w3, L0_ffn_gate_w):
    import jax
    import jax.numpy as jnp

    def _L0_xattn_ref(q_in, k_v, Wq, bq, Wk, bk, Wv, bv):
        import jax, jax.numpy as jnp
        import numpy as np
        EMBED = 128
        B, I, J = (8, 256, 256)
        SCALE = EMBED ** (-0.5)
        q = q_in @ Wq + bq
        k = k_v @ Wk + bk
        v = k_v @ Wv + bv
        sim = jnp.einsum('bid,bjd->bij', q, k) * SCALE
        attn = jax.nn.softmax(sim, axis=-1)
        out = jnp.einsum('bij,bjd->bid', attn, v)
        return out

    def _L0_ffn_ref(x, w12, w3, gate_w):
        import jax, jax.numpy as jnp
        import numpy as np
        TOP_K = 2
        E = gate_w.shape[0]
        H = w3.shape[-1]
        scores = jnp.einsum('btd,ed->bte', x, gate_w)
        topk_scores, topk_idx = jax.lax.top_k(scores, TOP_K)
        topk_probs = jax.nn.softmax(topk_scores, axis=-1)
        total_probs = jnp.sum(jax.nn.one_hot(topk_idx, E, dtype=topk_probs.dtype) * topk_probs[..., None], axis=-2)
        h12 = jnp.einsum('btd,ehd->bteh', x, w12)
        h1, h2 = (h12[..., :H], h12[..., H:])
        hidden = jax.nn.silu(h1) * h2
        expert_out = jnp.einsum('bteh,edh->bted', hidden, w3)
        y = jnp.sum(total_probs[..., None] * expert_out, axis=-2)
        return y
    x = x + jnp.tanh(g_xattn[0]) * _L0_xattn_ref(_layernorm(x, axis=-1), ctx_1024, L0_xattn_Wq, L0_xattn_bq, L0_xattn_Wk, L0_xattn_bk, L0_xattn_Wv, L0_xattn_bv)
    x = x + jnp.tanh(g_ffn[0]) * _L0_ffn_ref(_layernorm(x, axis=-1), L0_ffn_w12, L0_ffn_w3, L0_ffn_gate_w)
    return x

_drawn_inputs = setup_inputs


def setup_inputs(seed=0):
    import zlib

    import numpy as np

    out = dict(_drawn_inputs(seed))
    spreads = {'L0_xattn_bq': (0.0, 0.1), 'L0_xattn_bk': (0.0, 0.1), 'L0_xattn_bv': (0.0, 0.1)}
    factors = {}
    for name, (base, spread) in spreads.items():
        noise = np.random.default_rng([zlib.crc32(name.encode()), seed]).standard_normal(out[name].shape)
        drawn = base * np.exp(spread * noise) if base else spread * noise
        out[name] = jnp.asarray(drawn.astype(out[name].dtype))
    for name, factor in factors.items():
        out[name] = (out[name] * factor).astype(out[name].dtype)
    return out
```

```python
import concourse.bass as bass
from concourse import mybir
from contextlib import ExitStack

F32 = mybir.dt.float32
F32R = mybir.dt.float32r
BF16 = mybir.dt.bfloat16
ALU = mybir.AluOpType
ACT = mybir.ActivationFunctionType
AX = mybir.AxisListType

P = 128
B = 2
T = 4
TOK = P * T
D = 128
J = 77
E = 8
HALVES = 2 * E
WCOL = 3 * P
EPS = 1e-5
SCALE = float(D) ** -0.5
LOWEST = -3.0e38

C_WQT, C_WK, C_WV, C_GATE = 0, D, 2 * D, 3 * D
C_BQ = C_GATE + E
C_BK = C_BQ + 1
C_GX = C_BK + 1
C_GF = C_GX + 1
C_BV = C_GF + 1
C_CTX = C_BV + D
PARAMS = C_CTX + B * J

PER = 8
TURNS = 2 * HALVES // PER
SLOTS = 4
LAG = 3
AHEAD = 2


def build(nc, x, params, weights, out):
    x_rows = x.rearrange("b (p i) d -> b p i d", i=T)
    out_rows = out.rearrange("b (p i) d -> b p i d", i=T)

    with ExitStack() as ctx:
        def sb(name, shape, dt=F32):
            return ctx.enter_context(nc.sbuf_tensor(name, shape, dt))

        def bank(name):
            return ctx.enter_context(nc.psum_tensor(name, [P, 512], F32))

        def sem(name):
            return ctx.enter_context(nc.semaphore(name))

        par = sb("par", [P, PARAMS])
        w_raw = sb("w_raw", [P, HALVES + AHEAD, WCOL])
        w_hi = sb("w_hi", [P, SLOTS, WCOL], F32R)
        w_lo = sb("w_lo", [P, SLOTS, WCOL], F32R)
        x_in = sb("x_in", [P, B, T, D])
        ident = sb("ident", [P, P])
        ident16 = sb("ident16", [P, P], BF16)
        ones_row = sb("ones_row", [1, P])
        zeros_r = sb("zeros_r", [P, 512], F32R)
        minus_half = sb("minus_half", [P, T])
        prefer = sb("prefer", [P, T, E])
        pick = sb("pick", [P, E, P], BF16)
        gates = sb("gates", [P, 2])
        gate_hi = sb("gate_hi", [P, E], F32R)
        gate_lo = sb("gate_lo", [P, E], F32R)
        k_col = sb("k_col", [P, B * J])
        a_col = sb("a_col", [P, B * J])
        c_row = sb("c_row", [1, B * J])
        v_row = sb("v_row", [J, B, D])
        stats = sb("stats", [P, 2 * B, T, 6])
        moments = sb("moments", [P, 2 * B, T, 2])
        var_eps = sb("var_eps", [P, 2 * B, T])
        rstd = sb("rstd", [P, 2 * B, T])
        x_n = sb("x_n", [P, 2 * B, T, D])
        xn_col = sb("xn_col", [P, B, TOK])
        top = sb("top", [P, B, T])
        shifted = sb("shifted", [P, B, T, J])
        e_row = sb("e_row", [P, B, T, J])
        e_sum = sb("e_sum", [P, B, T])
        e_scale = sb("e_scale", [P, B, T])
        e_inv = sb("e_inv", [P, B, T])
        e_col = sb("e_col", [J, B, TOK])
        x2 = sb("x2", [P, B, T, D])
        x2_hi = sb("x2_hi", [P, B, TOK], F32R)
        x2_lo = sb("x2_lo", [P, B, TOK], F32R)
        sc = sb("sc", [P, B, T, E])
        sc2 = sb("sc2", [P, B, T, E])
        eq = sb("eq", [P, 2 * B, T, E])
        cand = sb("cand", [P, 2 * B, T, E])
        best = sb("best", [P, 2 * B, T])
        found = sb("found", [P, 2 * B, T])
        hot = sb("hot", [P, 2 * B, T, E])
        diff = sb("diff", [P, B, T])
        ex = sb("ex", [P, B, T])
        den = sb("den", [P, B, T])
        inv = sb("inv", [P, B, T])
        p1 = sb("p1", [P, B, T])
        p2 = sb("p2", [P, B, T])
        pr1 = sb("pr1", [P, B, T, E])
        pr2 = sb("pr2", [P, B, T, E])
        prob = sb("prob", [P, B, T, E])
        rest = sb("rest", [P, B, T, E])
        prob16 = sb("prob16", [P, B, T, 3, E], BF16)
        prob_col = sb("prob_col", [P, B, TOK], BF16)
        silu = sb("silu", [P, SLOTS, TOK])
        glu = sb("glu", [P, SLOTS, TOK])
        hid = sb("hid", [P, SLOTS, TOK])
        hid_hi = sb("hid_hi", [P, SLOTS, TOK], F32R)
        hid_lo = sb("hid_lo", [P, SLOTS, TOK], F32R)
        y_col = sb("y_col", [P, B, TOK])
        y_out = sb("y_out", [P, B, T, D])

        H1 = [bank("H1a"), bank("H1b")]
        H2 = [bank("H2a"), bank("H2b")]
        PB = [bank("PBa"), bank("PBb")]
        Y = [bank("Ya"), bank("Yb")]

        def tiles(b_, n=D):
            return b_[:, 0:T * n].rearrange("p (i n) -> p i n", n=n)

        ps_xn, ps_o, ps_fin = H1, H1, H1
        ps_sim, ps_x2 = H2, H2
        ps_e, ps_gate = PB, PB
        ps_k, ps_a, ps_v, ps_c = Y[0], Y[1], PB[1], PB[0]
        ps_prob = Y

        s_x = [sem("x_landed0"), sem("x_landed1")]
        s_par = sem("params_landed")
        s_w = [sem(f"weights_landed{q}") for q in range(4)]
        s_out = sem("out_written")
        s_const = sem("pool_consts")
        s_vconst = sem("vector_consts")
        s_gates = sem("gates_ready")
        s_kps, s_k, s_acv_ps, s_acv = sem("k_psum"), sem("k_ready"), sem("acv_psum"), sem("acv_ready")
        s_chain = sem("vector_chain")
        s_var = sem("variance_ready")
        s_rstd = sem("rstd_ready")
        s_xn = sem("normed_ready")
        s_xt = sem("transposed_psum")
        s_xc = sem("columns_ready")
        s_sim = sem("sim_psum")
        s_shift = sem("shifted_ready")
        s_exp = sem("exp_ready")
        s_et = sem("exp_transposed_psum")
        s_ec = sem("exp_columns_ready")
        s_o = sem("attended_psum")
        s_x2t = sem("x2_transposed_psum")
        s_xhi = sem("x2_hi_ready")
        s_xlo = sem("x2_lo_ready")
        s_sc = sem("gate_scores_psum")
        s_diff = sem("score_gap_ready")
        s_gap = sem("gap_exp_ready")
        s_p16 = sem("probs_ready")
        s_pt = sem("probs_transposed_psum")
        s_pc = sem("prob_columns_ready")
        s_h1, s_h2, s_pb = sem("h1_psum"), sem("h2_psum"), sem("probs_spread_psum")
        s_silu, s_glu, s_hid = sem("silu_ready"), sem("glu_ready"), sem("hidden_ready")
        s_hhi, s_hlo, s_y = sem("hidden_hi_ready"), sem("hidden_lo_ready"), sem("y_added")
        s_whi, s_wlo = sem("w_hi_ready"), sem("w_lo_ready")
        s_yc, s_yt, s_fin = sem("y_columns_ready"), sem("y_transposed_psum"), sem("result_ready")

        block = ctx.enter_context(nc.Block())

        @block.sync
        def _(sp):
            sp.dma_start(x_in[:, 0], x_rows[0]).then_inc(s_x[0], 16)
            sp.dma_start(x_in[:, 1], x_rows[1]).then_inc(s_x[1], 16)
            for q in range(4):
                sp.dma_start(w_raw[:, 4 * q:4 * q + 4], weights[:, 4 * q:4 * q + 4]).then_inc(s_w[q], 16)
            for b in range(B):
                sp.wait_ge(s_fin, b + 1)
                sp.dma_start(out_rows[b], y_out[:, b]).then_inc(s_out, 16)
            sp.wait_ge(s_out, 16 * B)

        @block.gpsimd
        def _(pool):
            pool.memset(ident[:], 0.0).then_inc(s_const, 1)
            pool.memset(minus_half[:], -0.5).then_inc(s_const, 1)
            pool.wait_ge(s_const, 2)
            pool.affine_select(out=ident[:], in_=ident[:], compare_op=ALU.not_equal, fill=1.0, base=0,
                               pattern=[[-1, P]], channel_multiplier=1).then_inc(s_const, 1)

            def power(k):
                pool.wait_ge(s_var, k + 1)
                pool.tensor_tensor(out=rstd[:, k], in0=var_eps[:, k], in1=minus_half[:], op=ALU.pow).then_inc(s_rstd, 1)

            power(0)
            power(1)
            pool.memset(ident16[:], 0.0).then_inc(s_const, 1)
            pool.memset(pick[:], 0.0).then_inc(s_const, 1)
            pool.iota(prefer[:], pattern=[[0, T], [-1, E]], base=E, channel_multiplier=0,
                      allow_small_or_imprecise_dtypes=True).then_inc(s_const, 1)
            pool.wait_ge(s_const, 6)
            pool.affine_select(out=ident16[:], in_=ident16[:], compare_op=ALU.not_equal, fill=1.0, base=0,
                               pattern=[[-1, P]], channel_multiplier=1).then_inc(s_const, 1)
            for part in range(3):
                if part:
                    pool.wait_ge(s_const, 7 + part)
                pool.affine_select(out=pick[:], in_=pick[:], compare_op=ALU.not_equal, fill=1.0,
                                   base=-E * part, pattern=[[-1, E], [0, P]], channel_multiplier=1).then_inc(s_const, 1)
            pool.memset(w_raw[:, HALVES:HALVES + AHEAD], 0.0).then_inc(s_const, 1)
            power(2)
            power(3)

            def low_part(n, k):
                pool.wait_ge(s_hhi, n + 1)
                if not isinstance(n, int) or n >= SLOTS:
                    pool.wait_ge(s_y, n - SLOTS + 1)
                pool.tensor_tensor(out=hid_lo[:, k], in0=hid[:, k], in1=hid_hi[:, k],
                                   op=ALU.subtract).then_inc(s_hlo, 1)

            for n in range(PER):
                low_part(n, n % SLOTS)
            with pool.Fori(1, TURNS) as turn:
                for n in range(PER):
                    low_part(turn * PER + n, n % SLOTS)

        @block.scalar
        def _(act):
            act.dma_start(par[:], params).then_inc(s_par, 16)
            act.wait_ge(s_par, 16)
            act.activation(gates[:], par[:, C_GX:C_GX + 2], ACT.Tanh).then_inc(s_gates, 1)
            act.wait_ge(s_kps, 1)
            act.activation(k_col[:], ps_k[:, 0:B * J], ACT.Identity, bias=par[:, C_BK:C_BK + 1]).then_inc(s_k, 1)
            act.wait_ge(s_acv_ps, 1)
            act.activation(a_col[:], ps_a[:, 0:B * J], ACT.Copy).then_inc(s_acv, 1)
            act.activation(c_row[:], ps_c[0:1, 0:B * J], ACT.Copy).then_inc(s_acv, 1)

            for b in range(B):
                act.wait_ge(s_xt, b + 1)
                act.activation(xn_col[:, b], ps_xn[b][:], ACT.Copy).then_inc(s_xc, 1)
            for b in range(B):
                act.wait_ge(s_shift, b + 1)
                act.activation(e_row[:, b], shifted[:, b], ACT.Exp, scale=SCALE).then_inc(s_exp, 1)
            for b in range(B):
                act.wait_ge(s_et, b + 1)
                act.activation(e_col[:, b], ps_e[b][0:J, :], ACT.Copy).then_inc(s_ec, 1)
            for b in range(B):
                act.wait_ge(s_x2t, b + 1)
                act.activation(x2_hi[:, b], ps_x2[b][:], ACT.Copy).then_inc(s_xhi, 1)

            def weights_hi(j, k):
                if not isinstance(j, int) or j >= SLOTS:
                    act.wait_ge(s_y, 2 * j - 2 * SLOTS + 2)
                act.activation(w_hi[:, k], w_raw[:, j], ACT.Copy).then_inc(s_whi, 1)

            def silu_step(n, k):
                act.wait_ge(s_h1, n + 1)
                if not isinstance(n, int) or n >= SLOTS:
                    act.wait_ge(s_glu, n - SLOTS + 1)
                act.activation(silu[:, k], H1[k % 2][:], ACT.Silu).then_inc(s_silu, 1)

            def hidden_hi(n, k):
                act.wait_ge(s_hid, n + 1)
                if not isinstance(n, int) or n >= SLOTS:
                    act.wait_ge(s_y, n - SLOTS + 1)
                act.activation(hid_hi[:, k], hid[:, k], ACT.Copy).then_inc(s_hhi, 1)

            act.wait_ge(s_w[0], 16)
            for j in range(AHEAD):
                weights_hi(j, j)
            for b in range(B):
                act.wait_ge(s_diff, b + 1)
                act.activation(ex[:, b], diff[:, b], ACT.Exp).then_inc(s_gap, 1)
            for q in range(1, 4):
                act.wait_ge(s_w[q], 16)
            act.wait_ge(s_const, 11)

            def turn_of_steps(n0, j0, first):
                for n in range(PER):
                    silu_step(n0 + n, n % SLOTS)
                    if not (first and n == 0):
                        hidden_hi(n0 + n - 1, (n - 1) % SLOTS)
                    if n % 2 == 1:
                        weights_hi(j0 + (n // 2 + AHEAD), (n // 2 + AHEAD) % SLOTS)

            turn_of_steps(0, 0, True)
            with act.Fori(1, TURNS) as turn:
                turn_of_steps(turn * PER, turn * (PER // 2), False)
            hidden_hi(2 * HALVES - 1, (2 * HALVES - 1) % SLOTS)
            for b in range(B):
                act.wait_ge(s_y, 2 * HALVES - 1 + b)
                act.activation(y_col[:, b], Y[b][:], ACT.Copy).then_inc(s_yc, 1)

        @block.vector
        def _(dve):
            links = [0]

            def chain(instruction):
                links[0] += 1
                instruction.then_inc(s_chain, 1)
                dve.wait_ge(s_chain, links[0])

            def note(instruction):
                links[0] += 1
                instruction.then_inc(s_chain, 1)

            def all_noted():
                dve.wait_ge(s_chain, links[0])

            dve.memset(ones_row[:], 1.0).then_inc(s_vconst, 1)
            dve.memset(prob_col[:], 0.0).then_inc(s_vconst, 1)
            dve.memset(zeros_r[:].bitcast(F32), 0.0).then_inc(s_vconst, 1)

            def row_stats(k, rows):
                for i in range(T):
                    note(dve.bn_stats(stats[:, k, i], rows[:, i]))
                all_noted()
                for i in range(T):
                    note(dve.bn_aggr(moments[:, k, i], stats[:, k, i]))
                all_noted()
                dve.tensor_scalar_add(var_eps[:, k], moments[:, k, :, 1], EPS).then_inc(s_var, 1)

            def normalise(k, rows):
                dve.wait_ge(s_rstd, k + 1)
                for i in range(T):
                    last = dve.tensor_scalar(x_n[:, k, i], rows[:, i], moments[:, k, i, 0:1], rstd[:, k, i:i + 1],
                                             ALU.subtract, ALU.mult)
                last.then_inc(s_xn, 1)

            for b in range(B):
                dve.wait_ge(s_x[b], 16)
                row_stats(b, x_in[:, b])
            dve.wait_ge(s_par, 16)
            chain(dve.tensor_copy(gate_hi[:], par[:, C_GATE:C_GATE + E]))
            note(dve.tensor_tensor(gate_lo[:], par[:, C_GATE:C_GATE + E], gate_hi[:].bitcast(F32), ALU.subtract))
            normalise(0, x_in[:, 0])
            normalise(1, x_in[:, 1])
            dve.wait_ge(s_acv_ps, 1)
            for b in range(B):
                last = dve.tensor_tensor(v_row[:, b], ps_v[0:J, b * D:(b + 1) * D], par[0:J, C_BV:C_BV + D], ALU.add)
            last.then_inc(s_acv, 1)

            for b in range(B):
                dve.wait_ge(s_sim, b + 1)
                sim = tiles(ps_sim[b], J)
                chain(dve.reduce_max(top[:, b], sim, AX.X))
                dve.tensor_tensor(shifted[:, b], sim, top[:, b].unsqueeze(2).broadcast_to([P, T, J]),
                                  ALU.subtract).then_inc(s_shift, 1)
            dve.wait_ge(s_gates, 1)
            for b in range(B):
                dve.wait_ge(s_exp, b + 1)
                chain(dve.reduce_sum(e_sum[:, b], e_row[:, b], AX.X))
                chain(dve.reciprocal(e_inv[:, b], e_sum[:, b]))
                chain(dve.tensor_scalar(e_scale[:, b], e_inv[:, b], gates[:, 0:1], None, ALU.mult))
            for b in range(B):
                dve.wait_ge(s_o, b + 1)
                for i in range(T):
                    note(dve.scalar_tensor_tensor(out=x2[:, b, i], in0=tiles(ps_o[b])[:, i], scalar=e_scale[:, b, i:i + 1],
                                                  in1=x_in[:, b, i], op0=ALU.mult, op1=ALU.add))
                all_noted()
                row_stats(B + b, x2[:, b])
            for b in range(B):
                normalise(B + b, x2[:, b])
            for b in range(B):
                dve.wait_ge(s_xhi, b + 1)
                dve.tensor_tensor(x2_lo[:, b], ps_x2[b][:], x2_hi[:, b].bitcast(F32), ALU.subtract).then_inc(s_xlo, 1)

            def weights_lo(j, k):
                dve.wait_ge(s_whi, j + 1)
                if not isinstance(j, int) or j >= SLOTS:
                    dve.wait_ge(s_y, 2 * j - 2 * SLOTS + 2)
                dve.tensor_tensor(w_lo[:, k], w_raw[:, j], w_hi[:, k].bitcast(F32), ALU.subtract).then_inc(s_wlo, 1)

            for j in range(AHEAD):
                weights_lo(j, j)

            dve.wait_ge(s_const, 6)
            for b in range(B):
                dve.wait_ge(s_sc, b + 1)
                chain(dve.tensor_copy(sc[:, b], tiles(ps_gate[b], E)))
                for r in range(2):
                    k = 2 * b + r
                    scores = (sc, sc2)[r][:, b]
                    chain(dve.reduce_max(best[:, k], scores, AX.X))
                    chain(dve.tensor_tensor(eq[:, k], scores, best[:, k].unsqueeze(2).broadcast_to([P, T, E]), ALU.is_equal))
                    chain(dve.tensor_tensor(cand[:, k], eq[:, k], prefer[:], ALU.mult))
                    chain(dve.reduce_max(found[:, k], cand[:, k], AX.X))
                    chain(dve.tensor_tensor(hot[:, k], prefer[:], found[:, k].unsqueeze(2).broadcast_to([P, T, E]), ALU.is_equal))
                    if r == 0:
                        chain(dve.scalar_tensor_tensor(out=sc2[:, b], in0=hot[:, k], scalar=LOWEST, in1=sc[:, b],
                                                       op0=ALU.mult, op1=ALU.add))
                dve.tensor_tensor(diff[:, b], best[:, 2 * b + 1], best[:, 2 * b], ALU.subtract).then_inc(s_diff, 1)
            for b in range(B):
                dve.wait_ge(s_gap, b + 1)
                chain(dve.tensor_scalar_add(den[:, b], ex[:, b], 1.0))
                chain(dve.reciprocal(inv[:, b], den[:, b]))
                chain(dve.tensor_scalar(p1[:, b], inv[:, b], gates[:, 1:2], None, ALU.mult))
                note(dve.tensor_tensor(p2[:, b], p1[:, b], ex[:, b], ALU.mult))
                note(dve.tensor_tensor(pr1[:, b], hot[:, 2 * b], p1[:, b].unsqueeze(2).broadcast_to([P, T, E]), ALU.mult))
                all_noted()
                chain(dve.tensor_tensor(pr2[:, b], hot[:, 2 * b + 1], p2[:, b].unsqueeze(2).broadcast_to([P, T, E]), ALU.mult))
                chain(dve.tensor_tensor(prob[:, b], pr1[:, b], pr2[:, b], ALU.add))
                chain(dve.tensor_copy(prob16[:, b, :, 0], prob[:, b]))
                chain(dve.tensor_tensor(rest[:, b], prob[:, b], prob16[:, b, :, 0], ALU.subtract))
                chain(dve.tensor_copy(prob16[:, b, :, 1], rest[:, b]))
                dve.tensor_tensor(prob16[:, b, :, 2], rest[:, b], prob16[:, b, :, 1], ALU.subtract).then_inc(s_p16, 1)
            for b in range(B):
                dve.wait_ge(s_pt, b + 1)
                dve.tensor_copy(prob_col[0:3 * E, b], ps_prob[b][0:3 * E, 0:TOK // 2].bitcast(BF16)).then_inc(s_pc, 1)

            def glu_step(n, k, pb):
                dve.wait_ge(s_silu, n + 1)
                dve.wait_ge(s_h2, n + 1)
                dve.tensor_tensor(glu[:, k], silu[:, k], H2[k % 2][:], ALU.mult).then_inc(s_glu, 1)
                dve.wait_ge(s_glu, n + 1)
                dve.wait_ge(s_pb, pb)
                if not isinstance(n, int) or n >= SLOTS:
                    dve.wait_ge(s_hlo, n - SLOTS + 1)
                dve.tensor_tensor(hid[:, k], glu[:, k], PB[k % 2][:], ALU.mult).then_inc(s_hid, 1)

            def turn_of_steps(n0, j0):
                for n in range(PER):
                    glu_step(n0 + n, n % SLOTS, j0 + (2 * (n // 4) + n % 2 + 1))
                    if n % 2 == 1:
                        weights_lo(j0 + (n // 2 + AHEAD), (n // 2 + AHEAD) % SLOTS)

            turn_of_steps(0, 0)
            with dve.Fori(1, TURNS) as turn:
                turn_of_steps(turn * PER, turn * (PER // 2))
            for b in range(B):
                dve.wait_ge(s_yt, b + 1)
                dve.tensor_tensor(y_out[:, b], x2[:, b], tiles(ps_fin[b]), ALU.add).then_inc(s_fin, 1)

        @block.tensor
        def _(pe):
            pe.wait_ge(s_par, 16)
            ctx_col = par[:, C_CTX:C_CTX + B * J]
            pe.matmul(ps_k[:, 0:B * J], par[:, C_WK:C_WK + D], ctx_col, start=True, stop=True).then_inc(s_kps, 1)
            for b in range(B):
                pe.matmul(ps_v[0:J, b * D:(b + 1) * D], ctx_col[:, b * J:(b + 1) * J], par[:, C_WV:C_WV + D],
                          start=True, stop=True)
            pe.wait_ge(s_k, 1)
            pe.matmul(ps_c[0:1, 0:B * J], par[:, C_BQ:C_BQ + 1], k_col[:], start=True, stop=True)
            pe.matmul(ps_a[:, 0:B * J], par[:, C_WQT:C_WQT + D], k_col[:], start=True, stop=True).then_inc(s_acv_ps, 1)

            pe.wait_ge(s_const, 3)
            for b in range(B):
                pe.wait_ge(s_xn, b + 1)
                for i in range(T):
                    last = pe.transpose(tiles(ps_xn[b])[:, i], x_n[:, b, i], ident[:])
                last.then_inc(s_xt, 1)
            pe.wait_ge(s_acv, 3)
            pe.wait_ge(s_vconst, 1)
            for b in range(B):
                pe.wait_ge(s_xc, b + 1)
                for i in range(T):
                    sim = tiles(ps_sim[b], J)[:, i]
                    pe.matmul(sim, xn_col[:, b, i * P:(i + 1) * P], a_col[:, b * J:(b + 1) * J], start=True, stop=False)
                    last = pe.matmul(sim, ones_row[:], c_row[:, b * J:(b + 1) * J], start=False, stop=True)
                last.then_inc(s_sim, 1)
            for b in range(B):
                pe.wait_ge(s_exp, b + 1)
                for i in range(T):
                    last = pe.transpose(tiles(ps_e[b])[0:J, i], e_row[:, b, i], ident[:])
                last.then_inc(s_et, 1)
            for b in range(B):
                pe.wait_ge(s_ec, b + 1)
                for i in range(T):
                    last = pe.matmul(tiles(ps_o[b])[:, i], e_col[:, b, i * P:(i + 1) * P], v_row[:, b], start=True, stop=True)
                last.then_inc(s_o, 1)
            for b in range(B):
                pe.wait_ge(s_xn, B + b + 1)
                for i in range(T):
                    last = pe.transpose(tiles(ps_x2[b])[:, i], x_n[:, B + b, i], ident[:])
                last.then_inc(s_x2t, 1)
            for b in range(B):
                pe.wait_ge(s_xlo, b + 1)
                for i in range(T):
                    gate = tiles(ps_gate[b], E)[:, i]
                    cols = slice(i * P, (i + 1) * P)
                    pe.matmul(gate, x2_hi[:, b, cols], gate_hi[:], start=True, stop=False)
                    pe.matmul(gate, x2_hi[:, b, cols], gate_lo[:], start=False, stop=False)
                    last = pe.matmul(gate, x2_lo[:, b, cols], gate_hi[:], start=False, stop=True)
                last.then_inc(s_sc, 1)

            def up(n, j, k, jk):
                b = k % 2
                if b == 0:
                    pe.wait_ge(s_wlo, j + 1)
                if not isinstance(n, int) or n >= 2:
                    pe.wait_ge(s_glu, n - 1)
                for part, (bank_, ready) in enumerate(((H1[b], s_h1), (H2[b], s_h2))):
                    cols = slice(part * P, (part + 1) * P)
                    pe.matmul(bank_[:], w_hi[:, jk, cols], x2_hi[:, b], start=True, stop=False)
                    pe.matmul(bank_[:], w_hi[:, jk, cols], x2_lo[:, b], start=False, stop=False)
                    pe.matmul(bank_[:], w_lo[:, jk, cols], x2_hi[:, b], start=False, stop=True).then_inc(ready, 1)

            def spread(n, e, b):
                if not isinstance(n, int) or n >= 2:
                    pe.wait_ge(s_hid, n - 1)
                pe.matmul(PB[b][:], pick[:, e], prob_col[:, b], start=True, stop=True).then_inc(s_pb, 1)

            def down(n, k, jk):
                b = k % 2
                cols = slice(2 * P, 3 * P)
                pe.wait_ge(s_hlo, n + 1)
                pe.matmul(Y[b][:], w_hi[:, jk, cols], hid_hi[:, k], start=False, stop=False, skip_group_check=True)
                pe.matmul(Y[b][:], w_hi[:, jk, cols], hid_lo[:, k], start=False, stop=False, skip_group_check=True)
                pe.matmul(Y[b][:], w_lo[:, jk, cols], hid_hi[:, k], start=False, stop=True,
                          skip_group_check=True).then_inc(s_y, 1)

            def probs_to_columns(b):
                pe.wait_ge(s_p16, b + 1)
                for i in range(T):
                    last = pe.transpose(ps_prob[b][0:3 * E, i * P // 2:(i + 1) * P // 2].bitcast(BF16),
                                        prob16[:, b, i].rearrange("p a e -> p (a e)"), ident16[:])
                last.then_inc(s_pt, 1)

            def turn_of_steps(n0, j0, e0, first):
                for n in range(PER):
                    up(n0 + n, j0 + n // 2, n % SLOTS, (n // 2) % SLOTS)
                    if first and n == 0:
                        pe.wait_ge(s_const, 10)
                        for b in range(B):
                            probs_to_columns(b)
                        for b in range(B):
                            pe.wait_ge(s_pc, b + 1)
                    if n % 4 < 2:
                        spread(n0 + n, e0 + n // 4, n % 2)
                    if first and n == 0:
                        pe.wait_ge(s_vconst, 3)
                        for b in range(B):
                            pe.matmul(Y[b][:], zeros_r[:, 0:P], zeros_r[:], start=True, stop=False, skip_group_check=True)
                    if not (first and n < LAG):
                        m = n - LAG
                        down(n0 + m, m % SLOTS, (m // 2) % SLOTS)

            turn_of_steps(0, 0, 0, True)
            with pe.Fori(1, TURNS) as turn:
                turn_of_steps(turn * PER, turn * (PER // 2), turn * (PER // 4), False)
            for n in range(2 * HALVES - LAG, 2 * HALVES):
                down(n, n % SLOTS, (n // 2) % SLOTS)
            for b in range(B):
                pe.wait_ge(s_yc, b + 1)
                for i in range(T):
                    last = pe.transpose(tiles(ps_fin[b])[:, i], y_col[:, b, i * P:(i + 1) * P], ident[:])
                last.then_inc(s_yt, 1)


def kernel(x, ctx_1024, g_xattn, g_ffn, L0_xattn_Wq, L0_xattn_bq, L0_xattn_Wk, L0_xattn_bk, L0_xattn_Wv,
           L0_xattn_bv, L0_ffn_w12, L0_ffn_w3, L0_ffn_gate_w):
    import numpy as np
    import concourse.bacc as bacc
    from concourse.bass_utils import run_bass_kernel_spmd

    columns = [
        np.transpose(L0_xattn_Wq), L0_xattn_Wk, L0_xattn_Wv, np.transpose(L0_ffn_gate_w),
        np.reshape(L0_xattn_bq, (D, 1)), np.reshape(L0_xattn_bk, (D, 1)),
        np.broadcast_to(np.reshape(g_xattn, (1, 1)), (D, 1)), np.broadcast_to(np.reshape(g_ffn, (1, 1)), (D, 1)),
        np.broadcast_to(np.reshape(L0_xattn_bv, (1, D)), (D, D)),
        np.reshape(np.transpose(ctx_1024, (2, 0, 1)), (D, B * J)),
    ]
    w12 = np.reshape(L0_ffn_w12, (E, 2, 2, P, D))
    w12 = np.transpose(w12, (4, 0, 2, 1, 3))
    w3 = np.transpose(np.reshape(L0_ffn_w3, (E, D, 2, P)), (3, 0, 2, 1))
    weights = np.concatenate([np.reshape(w12, (P, HALVES, 2 * P)), np.reshape(w3, (P, HALVES, P))], axis=2)
    arrays = {
        "x": np.ascontiguousarray(x),
        "params": np.ascontiguousarray(np.concatenate(columns, axis=1)),
        "weights": np.ascontiguousarray(weights),
    }
    nc = bacc.Bacc("TRN2", target_bir_lowering=False, num_devices=1)
    aps = [nc.dram_tensor(name, a.shape, mybir.dt.from_np(a.dtype), kind="ExternalInput").ap()
           for name, a in arrays.items()]
    out = nc.dram_tensor("out", (B, TOK, D), F32, kind="ExternalOutput").ap()
    build(nc, *aps, out)
    result = run_bass_kernel_spmd(nc, [arrays], core_ids=[0])
    return result.results[0]["out"]
```

```python
import concourse.bass as bass
from concourse import mybir
from contextlib import ExitStack

F32 = mybir.dt.float32
F32R = mybir.dt.float32r
BF16 = mybir.dt.bfloat16
U32 = mybir.dt.uint32
ALU = mybir.AluOpType
ACT = mybir.ActivationFunctionType
AX = mybir.AxisListType

P = 128
B = 2
T = 4
TOK = P * T
D = 128
J = 77
E = 8
HALVES = 2 * E
WCOL = 3 * P
EPS = 1e-5
SCALE = float(D) ** -0.5

C_WQT, C_WK, C_WV, C_GATE = 0, D, 2 * D, 3 * D
C_BQ = C_GATE + E
C_BK = C_BQ + 1
C_GX = C_BK + 1
C_GF = C_GX + 1
C_BV = C_GF + 1
C_CTX = C_BV + D
PARAMS = C_CTX + B * J

PER = 8
TURNS = 2 * HALVES // PER
SLOTS = 4
LAG = 3
AHEAD = 3


def build(nc, x, params, weights, out):
    x_rows = x.rearrange("b (p i) d -> b p i d", i=T)
    out_rows = out.rearrange("b (p i) d -> b p i d", i=T)

    with ExitStack() as ctx:
        def sb(name, shape, dt=F32):
            return ctx.enter_context(nc.sbuf_tensor(name, shape, dt))

        def bank(name):
            return ctx.enter_context(nc.psum_tensor(name, [P, 512], F32))

        def sem(name):
            return ctx.enter_context(nc.semaphore(name))

        par = sb("par", [P, PARAMS])
        w_raw = sb("w_raw", [P, HALVES + AHEAD, WCOL])
        w12_hi = sb("w12_hi", [P, SLOTS, 2 * P], F32R)
        w12_lo = sb("w12_lo", [P, SLOTS, 2 * P], F32R)
        w3_hi = sb("w3_hi", [P, SLOTS, P], F32R)
        w3_lo = sb("w3_lo", [P, SLOTS, P], F32R)
        x_in = sb("x_in", [P, B, T, D])
        ident = sb("ident", [P, P])
        ident16 = sb("ident16", [P, P], BF16)
        zeros_r = sb("zeros_r", [P, TOK], F32R)
        minus_half = sb("minus_half", [P, T])
        number = sb("number", [P, T, 2, E])
        pick = sb("pick", [P, E, P], BF16)
        gates = sb("gates", [P, 2])
        half_gate = sb("half_gate", [P, 2])
        gate_hi = sb("gate_hi", [P, E], F32R)
        gate_lo = sb("gate_lo", [P, E], F32R)
        wq_stats = sb("wq_stats", [P, 6])
        wq_mean = sb("wq_mean", [P, 2])
        wq_centred = sb("wq_centred", [P, D])
        k_col = sb("k_col", [P, B * J])
        a_col = sb("a_col", [P, B * J])
        c_all = sb("c_all", [P, B, J])
        v_row = sb("v_row", [J, B, D])
        stats = sb("stats", [P, 2 * B, T, 6])
        moments = sb("moments", [P, 2 * B, T, 2])
        var_eps = sb("var_eps", [P, 2 * B, T])
        rstd = sb("rstd", [P, 2 * B, T])
        x_col = sb("x_col", [P, B, TOK])
        sim = sb("sim", [P, B, T, J])
        top = sb("top", [P, B, T])
        shifted = sb("shifted", [P, B, T, J])
        e_row = sb("e_row", [P, B, T, J])
        e_sum = sb("e_sum", [P, B, T])
        e_scale = sb("e_scale", [P, B, T])
        e_inv = sb("e_inv", [P, B, T])
        e_col = sb("e_col", [J, B, TOK])
        x2 = sb("x2", [P, B, T, D])
        x2_n = sb("x2_n", [P, B, T, D])
        x2_hi = sb("x2_hi", [P, B, TOK], F32R)
        x2_lo = sb("x2_lo", [P, B, TOK], F32R)
        sc = sb("sc", [P, B, T, E])
        best = sb("best", [P, B, T, E])
        which = sb("which", [P, B, T, E], U32)
        hot = sb("hot", [P, B, T, 2, E])
        diff = sb("diff", [P, B, T])
        half_tanh = sb("half_tanh", [P, B, T])
        p12 = sb("p12", [P, B, T, 2])
        pr = sb("pr", [P, B, T, 2, E])
        prob = sb("prob", [P, B, T, E])
        rest = sb("rest", [P, B, T, E])
        prob16 = sb("prob16", [P, B, T, 3, E], BF16)
        prob_col = sb("prob_col", [P, B, TOK], BF16)
        silu = sb("silu", [P, SLOTS, TOK])
        glu = sb("glu", [P, SLOTS, TOK])
        hid = sb("hid", [P, SLOTS, TOK])
        hid_hi = sb("hid_hi", [P, SLOTS, TOK], F32R)
        hid_lo = sb("hid_lo", [P, SLOTS, TOK], F32R)
        y_col = sb("y_col", [P, B, TOK])
        y_out = sb("y_out", [P, B, T, D])

        H1 = [bank("H1a"), bank("H1b")]
        H2 = [bank("H2a"), bank("H2b")]
        PB = [bank("PBa"), bank("PBb")]
        Y = [bank("Ya"), bank("Yb")]

        def tiles(b_, n=D):
            return b_[:, 0:T * n].rearrange("p (i n) -> p i n", n=n)

        ps_k, ps_a, ps_c, ps_v = Y[0], Y[1], PB[0], PB[1]
        ps_x, ps_sim, ps_e = H1, H2, PB
        ps_o, ps_x2, ps_gate, ps_prob = Y, Y, Y, Y
        ps_fin = [H1[0], H2[0]]

        s_x = [sem("x_landed0"), sem("x_landed1")]
        s_par = sem("params_landed")
        s_w = [sem(f"weights_landed{q}") for q in range(4)]
        s_out = sem("out_written")
        s_const = sem("pool_consts")
        s_zeros = sem("zeros_ready")
        s_gates = sem("gates_ready")
        s_wq, s_kps, s_k = sem("wq_centred_ready"), sem("k_psum"), sem("k_ready")
        s_acv_ps, s_ac, s_v = sem("acv_psum"), sem("a_c_ready"), sem("v_ready")
        s_chain = sem("vector_chain")
        s_var, s_rstd = sem("variance_ready"), sem("rstd_ready")
        s_xt, s_xc = sem("x_transposed_psum"), sem("x_columns_ready")
        s_sim, s_shift, s_exp = sem("sim_psum"), sem("shifted_ready"), sem("exp_ready")
        s_et, s_ec, s_o = sem("exp_transposed_psum"), sem("exp_columns_ready"), sem("attended_psum")
        s_xn = sem("x2_normed_ready")
        s_x2t, s_xhi, s_xlo = sem("x2_transposed_psum"), sem("x2_hi_ready"), sem("x2_lo_ready")
        s_sc, s_diff, s_gap = sem("gate_scores_psum"), sem("score_gap_ready"), sem("gap_tanh_ready")
        s_p16, s_pt, s_pc = sem("probs_ready"), sem("probs_transposed_psum"), sem("prob_columns_ready")
        s_h1, s_h2, s_pb = sem("h1_psum"), sem("h2_psum"), sem("probs_spread_psum")
        s_silu, s_glu, s_hid = sem("silu_ready"), sem("glu_ready"), sem("hidden_ready")
        s_hhi, s_hlo, s_y = sem("hidden_hi_ready"), sem("hidden_lo_ready"), sem("y_added")
        s_w12hi, s_w12lo = sem("w12_hi_ready"), sem("w12_lo_ready")
        s_w3hi, s_w3lo = sem("w3_hi_ready"), sem("w3_lo_ready")
        s_yc, s_yt, s_fin = sem("y_columns_ready"), sem("y_transposed_psum"), sem("result_ready")

        def later(n, at_least):
            return not isinstance(n, int) or n >= at_least

        block = ctx.enter_context(nc.Block())

        @block.sync
        def _(sp):
            sp.dma_start(x_in[:, 0], x_rows[0]).then_inc(s_x[0], 16)
            sp.dma_start(x_in[:, 1], x_rows[1]).then_inc(s_x[1], 16)
            for q in range(4):
                sp.dma_start(w_raw[:, 4 * q:4 * q + 4], weights[:, 4 * q:4 * q + 4]).then_inc(s_w[q], 16)
            for b in range(B):
                sp.wait_ge(s_fin, b + 1)
                sp.dma_start(out_rows[b], y_out[:, b]).then_inc(s_out, 16)
            sp.wait_ge(s_out, 16 * B)

        @block.gpsimd
        def _(pool):
            pool.memset(ident[:], 0.0).then_inc(s_const, 1)
            pool.memset(minus_half[:], -0.5).then_inc(s_const, 1)
            pool.wait_ge(s_const, 2)
            pool.affine_select(out=ident[:], in_=ident[:], compare_op=ALU.not_equal, fill=1.0, base=0,
                               pattern=[[-1, P]], channel_multiplier=1).then_inc(s_const, 1)

            def power(k):
                pool.wait_ge(s_var, k + 1)
                pool.tensor_tensor(out=rstd[:, k], in0=var_eps[:, k], in1=minus_half[:], op=ALU.pow).then_inc(s_rstd, 1)

            power(0)
            power(1)
            pool.memset(ident16[:], 0.0).then_inc(s_const, 1)
            pool.memset(pick[:].rearrange("p e m -> p (e m)").bitcast(F32), 0.0).then_inc(s_const, 1)
            pool.iota(number[:], pattern=[[0, T], [0, 2], [1, E]], base=0, channel_multiplier=0,
                      allow_small_or_imprecise_dtypes=True).then_inc(s_const, 1)
            pool.wait_ge(s_const, 6)
            pool.affine_select(out=ident16[:], in_=ident16[:], compare_op=ALU.not_equal, fill=1.0, base=0,
                               pattern=[[-1, P]], channel_multiplier=1).then_inc(s_const, 1)
            for part in range(3):
                if part:
                    pool.wait_ge(s_const, 7 + part)
                pool.affine_select(out=pick[:], in_=pick[:], compare_op=ALU.not_equal, fill=1.0,
                                   base=-E * part, pattern=[[-1, E], [0, P]], channel_multiplier=1).then_inc(s_const, 1)
            pool.memset(w_raw[:, HALVES:HALVES + AHEAD], 0.0).then_inc(s_const, 1)
            power(2)
            power(3)

            def low_part(n, k):
                pool.wait_ge(s_hhi, n + 1)
                if later(n, SLOTS):
                    pool.wait_ge(s_y, n - SLOTS + 1)
                pool.tensor_tensor(out=hid_lo[:, k], in0=hid[:, k], in1=hid_hi[:, k],
                                   op=ALU.subtract).then_inc(s_hlo, 1)

            for n in range(PER):
                low_part(n, n % SLOTS)
            with pool.Fori(1, TURNS) as turn:
                for n in range(PER):
                    low_part(turn * PER + n, n % SLOTS)

        @block.scalar
        def _(act):
            act.dma_start(par[:], params).then_inc(s_par, 16)
            act.wait_ge(s_par, 16)
            act.activation(gates[:], par[:, C_GX:C_GX + 2], ACT.Tanh).then_inc(s_gates, 1)

            def x_columns(b):
                act.wait_ge(s_xt, b + 1)
                act.activation(x_col[:, b], ps_x[b][:], ACT.Copy).then_inc(s_xc, 1)

            def exps(b):
                act.wait_ge(s_shift, b + 1)
                act.activation(e_row[:, b], shifted[:, b], ACT.Exp, scale=SCALE).then_inc(s_exp, 1)

            def exp_columns(b):
                act.wait_ge(s_et, b + 1)
                act.activation(e_col[:, b], ps_e[b][0:J, :], ACT.Copy).then_inc(s_ec, 1)

            def x2_high(b):
                act.wait_ge(s_x2t, b + 1)
                act.activation(x2_hi[:, b], ps_x2[b][:], ACT.Copy).then_inc(s_xhi, 1)

            def gap(b):
                act.wait_ge(s_diff, b + 1)
                act.activation(half_tanh[:, b], diff[:, b], ACT.Tanh, scale=0.5).then_inc(s_gap, 1)

            def w12_high(h, k):
                act.activation(w12_hi[:, k], w_raw[:, h, 0:2 * P], ACT.Copy).then_inc(s_w12hi, 1)

            def w3_high(h, k):
                act.activation(w3_hi[:, k], w_raw[:, h, 2 * P:3 * P], ACT.Copy).then_inc(s_w3hi, 1)

            def silu_step(n, k):
                act.wait_ge(s_h1, n + 1)
                if later(n, SLOTS):
                    act.wait_ge(s_glu, n - SLOTS + 1)
                act.activation(silu[:, k], H1[k % 2][:], ACT.Silu).then_inc(s_silu, 1)

            def hidden_high(n, k):
                act.wait_ge(s_hid, n + 1)
                if later(n, SLOTS):
                    act.wait_ge(s_y, n - SLOTS + 1)
                act.activation(hid_hi[:, k], hid[:, k], ACT.Copy).then_inc(s_hhi, 1)

            x_columns(0)
            act.wait_ge(s_kps, 1)
            act.activation(k_col[:], ps_k[:, 0:B * J], ACT.Identity, bias=par[:, C_BK:C_BK + 1]).then_inc(s_k, 1)
            act.wait_ge(s_acv_ps, 1)
            act.activation(a_col[:], ps_a[:, 0:B * J], ACT.Copy).then_inc(s_ac, 1)
            act.activation(c_all[:].rearrange("p b j -> p (b j)"), ps_c[:, 0:B * J], ACT.Copy).then_inc(s_ac, 1)
            x_columns(1)
            exps(0)
            exps(1)
            exp_columns(0)
            exp_columns(1)
            act.wait_ge(s_w[0], 16)
            for h in range(AHEAD):
                w12_high(h, h)
            x2_high(0)
            x2_high(1)
            gap(0)
            for q in range(1, 4):
                act.wait_ge(s_w[q], 16)
            act.wait_ge(s_const, 11)

            def turn_of_steps(n0, h0, first):
                for n in range(PER):
                    silu_step(n0 + n, n % SLOTS)
                    if not (first and n == 0):
                        hidden_high(n0 + n - 1, (n - 1) % SLOTS)
                    if first and n == 1:
                        gap(1)
                    if n == 0:
                        if not first:
                            act.wait_ge(s_h2, n0)
                        w12_high(h0 + AHEAD, AHEAD)
                    if n < SLOTS:
                        if not first:
                            act.wait_ge(s_y, n0 + n - SLOTS + 1)
                        w3_high(h0 + n, n)
                    if n >= SLOTS + 1:
                        act.wait_ge(s_h2, n0 + n)
                        w12_high(h0 + n - 1, n - SLOTS - 1)

            turn_of_steps(0, 0, True)
            with act.Fori(1, TURNS) as turn:
                turn_of_steps(turn * PER, turn * (PER // 2), False)
            hidden_high(2 * HALVES - 1, (2 * HALVES - 1) % SLOTS)
            for b in range(B):
                act.wait_ge(s_y, 2 * HALVES - SLOTS * (B - 1 - b))
                act.activation(y_col[:, b], Y[b][:], ACT.Copy).then_inc(s_yc, 1)

        @block.vector
        def _(dve):
            links = [0]

            def note(instruction):
                links[0] += 1
                instruction.then_inc(s_chain, 1)

            def all_noted():
                dve.wait_ge(s_chain, links[0])

            def chain(instruction):
                note(instruction)
                all_noted()

            dve.memset(prob_col[:].rearrange("p b n -> p (b n)").bitcast(F32), 0.0).then_inc(s_zeros, 1)
            dve.memset(zeros_r[:].bitcast(F32), 0.0).then_inc(s_zeros, 1)

            def row_stats(k, rows):
                for i in range(T):
                    note(dve.bn_stats(stats[:, k, i], rows[:, i]))
                all_noted()
                for i in range(T):
                    note(dve.bn_aggr(moments[:, k, i], stats[:, k, i]))
                all_noted()
                dve.tensor_scalar_add(var_eps[:, k], moments[:, k, :, 1], EPS).then_inc(s_var, 1)

            def softmax_shift(b):
                dve.wait_ge(s_sim, b + 1)
                dve.wait_ge(s_rstd, b + 1)
                for i in range(T):
                    note(dve.scalar_tensor_tensor(out=sim[:, b, i], in0=tiles(ps_sim[b], J)[:, i],
                                                  scalar=rstd[:, b, i:i + 1], in1=c_all[:, b], op0=ALU.mult, op1=ALU.add))
                all_noted()
                chain(dve.reduce_max(top[:, b], sim[:, b], AX.X))
                dve.tensor_tensor(shifted[:, b], sim[:, b], top[:, b].unsqueeze(2).broadcast_to([P, T, J]),
                                  ALU.subtract).then_inc(s_shift, 1)

            def softmax_scale(b):
                dve.wait_ge(s_exp, b + 1)
                chain(dve.reduce_sum(e_sum[:, b], e_row[:, b], AX.X))
                chain(dve.reciprocal(e_inv[:, b], e_sum[:, b]))
                chain(dve.tensor_scalar(e_scale[:, b], e_inv[:, b], gates[:, 0:1], None, ALU.mult))

            def residual(b):
                dve.wait_ge(s_o, b + 1)
                for i in range(T):
                    note(dve.scalar_tensor_tensor(out=x2[:, b, i], in0=tiles(ps_o[b])[:, i], scalar=e_scale[:, b, i:i + 1],
                                                  in1=x_in[:, b, i], op0=ALU.mult, op1=ALU.add))
                all_noted()

            def normalise(b):
                dve.wait_ge(s_rstd, B + b + 1)
                for i in range(T):
                    last = dve.tensor_scalar(x2_n[:, b, i], x2[:, b, i], moments[:, B + b, i, 0:1],
                                             rstd[:, B + b, i:i + 1], ALU.subtract, ALU.mult)
                last.then_inc(s_xn, 1)

            def x2_low(b):
                dve.wait_ge(s_xhi, b + 1)
                dve.tensor_tensor(x2_lo[:, b], ps_x2[b][:], x2_hi[:, b].bitcast(F32), ALU.subtract).then_inc(s_xlo, 1)

            def best_two(b):
                dve.wait_ge(s_sc, b + 1)
                chain(dve.tensor_copy(sc[:, b], tiles(ps_gate[b], E)))
                for i in range(T):
                    note(dve.max(best[:, b, i], sc[:, b, i]))
                all_noted()
                for i in range(T):
                    note(dve.max_index(which[:, b, i], best[:, b, i], sc[:, b, i]))
                dve.tensor_tensor(diff[:, b], best[:, b, :, 1], best[:, b, :, 0], ALU.subtract).then_inc(s_diff, 1)
                all_noted()
                note(dve.tensor_tensor(hot[:, b], number[:], which[:, b, :, 0:2].unsqueeze(3).broadcast_to([P, T, 2, E]),
                                       ALU.is_equal))

            def probabilities(b):
                dve.wait_ge(s_gap, b + 1)
                for r in range(2):
                    note(dve.tensor_scalar(p12[:, b, :, r], half_tanh[:, b], half_gate[:, 1 - r:2 - r], half_gate[:, 0:1],
                                           ALU.mult, ALU.add))
                all_noted()
                chain(dve.tensor_tensor(pr[:, b], hot[:, b], p12[:, b].unsqueeze(3).broadcast_to([P, T, 2, E]), ALU.mult))
                chain(dve.tensor_tensor(prob[:, b], pr[:, b, :, 0], pr[:, b, :, 1], ALU.add))
                chain(dve.tensor_copy(prob16[:, b, :, 0], prob[:, b]))
                chain(dve.tensor_tensor(rest[:, b], prob[:, b], prob16[:, b, :, 0], ALU.subtract))
                chain(dve.tensor_copy(prob16[:, b, :, 1], rest[:, b]))
                dve.tensor_tensor(prob16[:, b, :, 2], rest[:, b], prob16[:, b, :, 1], ALU.subtract).then_inc(s_p16, 1)

            def prob_columns(b):
                dve.wait_ge(s_pt, b + 1)
                dve.tensor_copy(prob_col[0:3 * E, b], ps_prob[b][0:3 * E, 0:TOK // 2].bitcast(BF16)).then_inc(s_pc, 1)

            def w12_low(h, k):
                dve.wait_ge(s_w12hi, h + 1)
                dve.tensor_tensor(w12_lo[:, k], w_raw[:, h, 0:2 * P], w12_hi[:, k].bitcast(F32), ALU.subtract).then_inc(s_w12lo, 1)

            def w3_low(h, k):
                dve.wait_ge(s_w3hi, h + 1)
                dve.tensor_tensor(w3_lo[:, k], w_raw[:, h, 2 * P:3 * P], w3_hi[:, k].bitcast(F32), ALU.subtract).then_inc(s_w3lo, 1)

            dve.wait_ge(s_x[0], 16)
            row_stats(0, x_in[:, 0])
            dve.wait_ge(s_par, 16)
            chain(dve.bn_stats(wq_stats[:], par[:, C_WQT:C_WQT + D]))
            chain(dve.bn_aggr(wq_mean[:], wq_stats[:]))
            dve.tensor_scalar(wq_centred[:], par[:, C_WQT:C_WQT + D], wq_mean[:, 0:1], None, ALU.subtract).then_inc(s_wq, 1)
            dve.wait_ge(s_x[1], 16)
            row_stats(1, x_in[:, 1])
            note(dve.tensor_copy(gate_hi[:], par[:, C_GATE:C_GATE + E]))
            dve.wait_ge(s_gates, 1)
            note(dve.tensor_scalar(half_gate[:, 0:1], gates[:, 1:2], 0.5, None, ALU.mult))
            note(dve.tensor_scalar(half_gate[:, 1:2], gates[:, 1:2], -0.5, None, ALU.mult))
            all_noted()
            note(dve.tensor_tensor(gate_lo[:], par[:, C_GATE:C_GATE + E], gate_hi[:].bitcast(F32), ALU.subtract))
            dve.wait_ge(s_acv_ps, 1)
            for b in range(B):
                last = dve.tensor_tensor(v_row[:, b], ps_v[0:J, b * D:(b + 1) * D], par[0:J, C_BV:C_BV + D], ALU.add)
            last.then_inc(s_v, 1)
            dve.wait_ge(s_ac, 2)
            softmax_shift(0)
            softmax_shift(1)
            softmax_scale(0)
            softmax_scale(1)
            residual(0)
            row_stats(B, x2[:, 0])
            residual(1)
            normalise(0)
            row_stats(B + 1, x2[:, 1])
            x2_low(0)
            for h in range(AHEAD):
                w12_low(h, h)
            normalise(1)
            dve.wait_ge(s_const, 6)
            best_two(0)
            x2_low(1)
            probabilities(0)
            prob_columns(0)

            def glu_step(n, k, bank_):
                dve.wait_ge(s_silu, n + 1)
                dve.wait_ge(s_h2, n + 1)
                dve.tensor_tensor(glu[:, k], silu[:, k], H2[k % 2][:], ALU.mult).then_inc(s_glu, 1)

            def hidden_step(n, k, s):
                dve.wait_ge(s_glu, n + 1)
                dve.wait_ge(s_pb, s + 1)
                if later(n, SLOTS):
                    dve.wait_ge(s_hlo, n - SLOTS + 1)
                dve.tensor_tensor(hid[:, k], glu[:, k], PB[k // 2][:], ALU.mult).then_inc(s_hid, 1)

            def turn_of_steps(n0, h0, first):
                for n in range(PER):
                    glu_step(n0 + n, n % SLOTS, n // 2 % 2)
                    hidden_step(n0 + n, n % SLOTS, h0 + n // 2)
                    if first and n == 0:
                        best_two(1)
                    if n == 0:
                        w12_low(h0 + AHEAD, AHEAD)
                    if first and n == 1:
                        probabilities(1)
                    if first and n == 2:
                        prob_columns(1)
                    if n < SLOTS:
                        w3_low(h0 + n, n)
                    if n >= SLOTS + 1:
                        w12_low(h0 + n - 1, n - SLOTS - 1)

            turn_of_steps(0, 0, True)
            with dve.Fori(1, TURNS) as turn:
                turn_of_steps(turn * PER, turn * (PER // 2), False)
            for b in range(B):
                dve.wait_ge(s_yt, b + 1)
                dve.tensor_tensor(y_out[:, b], x2[:, b], tiles(ps_fin[b]), ALU.add).then_inc(s_fin, 1)

        @block.tensor
        def _(pe):
            def x_transposes(b):
                pe.wait_ge(s_x[b], 16)
                for i in range(T):
                    last = pe.transpose(tiles(ps_x[b])[:, i], x_in[:, b, i], ident[:])
                last.then_inc(s_xt, 1)

            def scores(b):
                pe.wait_ge(s_xc, b + 1)
                for i in range(T):
                    last = pe.matmul(tiles(ps_sim[b], J)[:, i], x_col[:, b, i * P:(i + 1) * P],
                                     a_col[:, b * J:(b + 1) * J], start=True, stop=True)
                last.then_inc(s_sim, 1)

            def exp_transposes(b):
                pe.wait_ge(s_exp, b + 1)
                for i in range(T):
                    last = pe.transpose(tiles(ps_e[b])[0:J, i], e_row[:, b, i], ident[:])
                last.then_inc(s_et, 1)

            def attend(b):
                pe.wait_ge(s_ec, b + 1)
                for i in range(T):
                    last = pe.matmul(tiles(ps_o[b])[:, i], e_col[:, b, i * P:(i + 1) * P], v_row[:, b], start=True, stop=True)
                last.then_inc(s_o, 1)

            def x2_transposes(b):
                pe.wait_ge(s_xn, b + 1)
                for i in range(T):
                    last = pe.transpose(tiles(ps_x2[b])[:, i], x2_n[:, b, i], ident[:])
                last.then_inc(s_x2t, 1)

            def gate_scores(b):
                pe.wait_ge(s_xlo, b + 1)
                for i in range(T):
                    gate = tiles(ps_gate[b], E)[:, i]
                    cols = slice(i * P, (i + 1) * P)
                    pe.matmul(gate, x2_hi[:, b, cols], gate_hi[:], start=True, stop=False)
                    pe.matmul(gate, x2_hi[:, b, cols], gate_lo[:], start=False, stop=False)
                    last = pe.matmul(gate, x2_lo[:, b, cols], gate_hi[:], start=False, stop=True)
                last.then_inc(s_sc, 1)

            def prob_transposes(b):
                pe.wait_ge(s_p16, b + 1)
                for i in range(T):
                    last = pe.transpose(ps_prob[b][0:3 * E, i * P // 2:(i + 1) * P // 2].bitcast(BF16),
                                        prob16[:, b, i].rearrange("p a e -> p (a e)"), ident16[:])
                last.then_inc(s_pt, 1)

            def y_zero(b):
                pe.wait_ge(s_pc, b + 1)
                pe.matmul(Y[b][:], zeros_r[:, 0:P], zeros_r[:], start=True, stop=False, skip_group_check=True)

            pe.wait_ge(s_const, 3)
            x_transposes(0)
            pe.wait_ge(s_par, 16)
            ctx_col = par[:, C_CTX:C_CTX + B * J]
            pe.matmul(ps_k[:, 0:B * J], par[:, C_WK:C_WK + D], ctx_col, start=True, stop=True).then_inc(s_kps, 1)
            for b in range(B):
                pe.matmul(ps_v[0:J, b * D:(b + 1) * D], ctx_col[:, b * J:(b + 1) * J], par[:, C_WV:C_WV + D],
                          start=True, stop=True)
            pe.wait_ge(s_k, 1)
            pe.wait_ge(s_wq, 1)
            pe.matmul(ps_a[:, 0:B * J], wq_centred[:], k_col[:], start=True, stop=True)
            pe.matmul(ps_c[:, 0:B * J], par[:, C_BQ:C_BQ + 1].broadcast_to([P, P]), k_col[:],
                      start=True, stop=True).then_inc(s_acv_ps, 1)
            x_transposes(1)
            pe.wait_ge(s_ac, 2)
            scores(0)
            scores(1)
            pe.wait_ge(s_v, 1)
            exp_transposes(0)
            exp_transposes(1)
            attend(0)
            attend(1)

            def up(n, h, k, b):
                if b == 0:
                    pe.wait_ge(s_w12lo, h + 1)
                if later(n, 2):
                    pe.wait_ge(s_glu, n - 1)
                for part, (bank_, ready) in enumerate(((H1[k % 2], s_h1), (H2[k % 2], s_h2))):
                    cols = slice(part * P, (part + 1) * P)
                    pe.matmul(bank_[:], w12_hi[:, k, cols], x2_hi[:, b], start=True, stop=False)
                    pe.matmul(bank_[:], w12_hi[:, k, cols], x2_lo[:, b], start=False, stop=False)
                    pe.matmul(bank_[:], w12_lo[:, k, cols], x2_hi[:, b], start=False, stop=True).then_inc(ready, 1)

            def spread(n, e, s, b):
                if later(n, SLOTS):
                    pe.wait_ge(s_hid, n - 2)
                pe.matmul(PB[s][:], pick[:, e], prob_col[:, b], start=True, stop=True).then_inc(s_pb, 1)

            def down(n, h, k, b):
                pe.wait_ge(s_hlo, n + 1)
                if b == 0:
                    pe.wait_ge(s_w3lo, h + 1)
                pe.matmul(Y[b][:], w3_hi[:, k], hid_hi[:, k], start=False, stop=False, skip_group_check=True)
                pe.matmul(Y[b][:], w3_hi[:, k], hid_lo[:, k], start=False, stop=False, skip_group_check=True)
                pe.matmul(Y[b][:], w3_lo[:, k], hid_hi[:, k], start=False, stop=True,
                          skip_group_check=True).then_inc(s_y, 1)

            def turn_of_steps(n0, h0, e0, first):
                for n in range(PER):
                    up(n0 + n, h0 + n % SLOTS, n % SLOTS, n // SLOTS)
                    if first and n == 0:
                        gate_scores(0)
                        x2_transposes(1)
                    if first and n == 1:
                        gate_scores(1)
                        prob_transposes(0)
                        y_zero(0)
                        spread(0, 0, 0, 0)
                    if first and n == 3:
                        prob_transposes(1)
                        y_zero(1)
                    if n % 2 == 0 and not (first and n == 0):
                        spread(n0 + n, e0 + n // 2 % 2, n // 2 % 2, n // SLOTS)
                    if not (first and n < LAG):
                        m = (n - LAG) % PER
                        down(n0 + (n - LAG), h0 + m % SLOTS, m % SLOTS, m // SLOTS)

            x2_transposes(0)
            pe.wait_ge(s_xlo, 1)
            pe.wait_ge(s_const, 10)
            pe.wait_ge(s_zeros, 2)
            turn_of_steps(0, 0, 0, True)
            with pe.Fori(1, TURNS) as turn:
                turn_of_steps(turn * PER, turn * (PER // 2), turn * (PER // 4), False)

            def y_transposes(b):
                pe.wait_ge(s_yc, b + 1)
                for i in range(T):
                    last = pe.transpose(tiles(ps_fin[b])[:, i], y_col[:, b, i * P:(i + 1) * P], ident[:])
                last.then_inc(s_yt, 1)

            for n in range(2 * HALVES - LAG, 2 * HALVES):
                down(n, HALVES - 2 * HALVES + n, n % SLOTS, 1)
                if n == 2 * HALVES - 2:
                    pe.wait_ge(s_glu, 2 * HALVES - 1)
                    y_transposes(0)
            y_transposes(1)


def kernel(x, ctx_1024, g_xattn, g_ffn, L0_xattn_Wq, L0_xattn_bq, L0_xattn_Wk, L0_xattn_bk, L0_xattn_Wv,
           L0_xattn_bv, L0_ffn_w12, L0_ffn_w3, L0_ffn_gate_w):
    import numpy as np
    import concourse.bacc as bacc
    from concourse.bass_utils import run_bass_kernel_spmd

    columns = [
        np.transpose(L0_xattn_Wq), L0_xattn_Wk, L0_xattn_Wv, np.transpose(L0_ffn_gate_w),
        np.reshape(L0_xattn_bq, (D, 1)), np.reshape(L0_xattn_bk, (D, 1)),
        np.broadcast_to(np.reshape(g_xattn, (1, 1)), (D, 1)), np.broadcast_to(np.reshape(g_ffn, (1, 1)), (D, 1)),
        np.broadcast_to(np.reshape(L0_xattn_bv, (1, D)), (D, D)),
        np.reshape(np.transpose(ctx_1024, (2, 0, 1)), (D, B * J)),
    ]
    w12 = np.reshape(L0_ffn_w12, (E, 2, 2, P, D))
    w12 = np.transpose(w12, (4, 0, 2, 1, 3))
    w3 = np.transpose(np.reshape(L0_ffn_w3, (E, D, 2, P)), (3, 0, 2, 1))
    weights = np.concatenate([np.reshape(w12, (P, HALVES, 2 * P)), np.reshape(w3, (P, HALVES, P))], axis=2)
    arrays = {
        "x": np.ascontiguousarray(x),
        "params": np.ascontiguousarray(np.concatenate(columns, axis=1)),
        "weights": np.ascontiguousarray(weights),
    }
    nc = bacc.Bacc("TRN2", target_bir_lowering=False, num_devices=1)
    aps = [nc.dram_tensor(name, a.shape, mybir.dt.from_np(a.dtype), kind="ExternalInput").ap()
           for name, a in arrays.items()]
    out = nc.dram_tensor("out", (B, TOK, D), F32, kind="ExternalOutput").ap()
    build(nc, *aps, out)
    result = run_bass_kernel_spmd(nc, [arrays], core_ids=[0])
    return result.results[0]["out"]
```

```python
import concourse.bass as bass
from concourse import mybir
from contextlib import ExitStack

F32 = mybir.dt.float32
F32R = mybir.dt.float32r
BF16 = mybir.dt.bfloat16
U32 = mybir.dt.uint32
ALU = mybir.AluOpType
ACT = mybir.ActivationFunctionType
AX = mybir.AxisListType

P = 128
B = 2
T = 4
TOK = P * T
D = 128
J = 77
E = 8
HALVES = 2 * E
WCOL = 3 * P
EPS = 1e-5
SCALE = float(D) ** -0.5

C_WQT, C_WK, C_WV, C_GATE = 0, D, 2 * D, 3 * D
C_BQ = C_GATE + E
C_BK = C_BQ + 1
C_GX = C_BK + 1
C_GF = C_GX + 1
C_BV = C_GF + 1
C_CTX = C_BV + D
PARAMS = C_CTX + B * J

PER = 8
SLOTS = 4
STEPS = 2 * HALVES
TURNS = STEPS // PER
LAG = 3
AHEAD = 3


LAST = (STEPS - 1) % SLOTS
HALF_COLS = [slice(0, TOK // 2), slice(TOK // 2, TOK)]
HALF_TILES = [slice(0, T // 2), slice(T // 2, T)]


def build(nc, x, params, weights, out):
    x_rows = x.rearrange("b (p i) d -> b p i d", i=T)
    out_rows = out.rearrange("b (p i) d -> b p i d", i=T)

    with ExitStack() as ctx:
        def sb(name, shape, dt=F32):
            return ctx.enter_context(nc.sbuf_tensor(name, shape, dt))

        def bank(name):
            return ctx.enter_context(nc.psum_tensor(name, [P, 512], F32))

        def sem(name):
            return ctx.enter_context(nc.semaphore(name))

        par = sb("par", [P, PARAMS])
        w_raw = sb("w_raw", [P, HALVES + AHEAD, WCOL])
        w12_hi = sb("w12_hi", [P, SLOTS, 2 * P], F32R)
        w12_lo = sb("w12_lo", [P, SLOTS, 2 * P], F32R)
        w3_hi = sb("w3_hi", [P, SLOTS, P], F32R)
        w3_lo = sb("w3_lo", [P, SLOTS, P], F32R)
        x_in = sb("x_in", [P, B, T, D])
        ident = sb("ident", [P, P])
        ident16 = sb("ident16", [P, P], BF16)
        zeros_r = sb("zeros_r", [P, TOK], F32R)
        minus_half = sb("minus_half", [P, T])
        table_load = sb("table_load", [P, T])
        number = sb("number", [P, T, 2, E])
        pick = sb("pick", [P, E, P], BF16)
        gates = sb("gates", [P, 2])
        half_gate = sb("half_gate", [P, 2])
        gate_hi = sb("gate_hi", [P, E], F32R)
        gate_lo = sb("gate_lo", [P, E], F32R)
        wq_stats = sb("wq_stats", [P, 6])
        wq_mean = sb("wq_mean", [P, 2])
        wq_centred = sb("wq_centred", [P, D])
        k_col = sb("k_col", [P, B * J])
        a_col = sb("a_col", [P, B * J])
        c_all = sb("c_all", [P, B, J])
        v_row = sb("v_row", [J, B, D])
        stats = sb("stats", [P, 2 * B, T, 6])
        moments = sb("moments", [P, 2 * B, T, 2])
        var_eps = sb("var_eps", [P, 2 * B, T])
        rstd = sb("rstd", [P, 2 * B, T])
        x_col = sb("x_col", [P, B, TOK])
        sim = sb("sim", [P, B, T, J])
        top = sb("top", [P, B, T])
        shifted = sb("shifted", [P, B, T, J])
        e_row = sb("e_row", [P, B, T, J])
        e_sum = sb("e_sum", [P, B, T])
        e_scale = sb("e_scale", [P, B, T])
        e_inv = sb("e_inv", [P, B, T])
        e_col = sb("e_col", [J, B, TOK])
        x2 = sb("x2", [P, B, T, D])
        x2_n = sb("x2_n", [P, B, T, D])
        x2_hi = sb("x2_hi", [P, B, TOK], F32R)
        x2_lo = sb("x2_lo", [P, B, TOK], F32R)
        sc = sb("sc", [P, B, T, E])
        best = sb("best", [P, B, T, E])
        which = sb("which", [P, B, T, E], U32)
        hot = sb("hot", [P, B, T, 2, E])
        diff = sb("diff", [P, B, T])
        half_tanh = sb("half_tanh", [P, B, T])
        p12 = sb("p12", [P, B, T, 2])
        pr = sb("pr", [P, B, T, 2, E])
        prob = sb("prob", [P, B, T, E])
        rest = sb("rest", [P, B, T, E])
        prob16 = sb("prob16", [P, B, T, 3, E], BF16)
        prob_col = sb("prob_col", [P, B, TOK], BF16)
        silu = sb("silu", [P, SLOTS, TOK])
        glu = sb("glu", [P, SLOTS, TOK])
        hid = sb("hid", [P, SLOTS, TOK])
        hid_hi = sb("hid_hi", [P, SLOTS, TOK], F32R)
        hid_lo = sb("hid_lo", [P, SLOTS, TOK], F32R)
        y_col = sb("y_col", [P, B, TOK])
        y_out = sb("y_out", [P, B, T, D])

        H1 = [bank("H1a"), bank("H1b")]
        H2 = [bank("H2a"), bank("H2b")]
        PB = [bank("PBa"), bank("PBb")]
        Y = [bank("Ya"), bank("Yb")]

        def tiles(b_, n=D):
            return b_[:, 0:T * n].rearrange("p (i n) -> p i n", n=n)

        ps_k, ps_a, ps_c, ps_v = Y[0], Y[1], PB[0], PB[1]
        ps_x, ps_sim, ps_e = H1, H2, PB
        ps_o, ps_x2, ps_gate, ps_prob = Y, Y, Y, Y
        ps_fin = [H1[0], H2[0], H1[1]]

        s_x = [sem("x_landed0"), sem("x_landed1")]
        s_par = sem("params_landed")
        s_w = [sem(f"weights_landed{q}") for q in range(4)]
        s_out = sem("out_written")
        s_const = sem("pool_consts")
        s_zeros = sem("zeros_ready")
        s_gates = sem("gates_ready")
        s_wq, s_kps, s_k = sem("wq_centred_ready"), sem("k_psum"), sem("k_ready")
        s_acv_ps, s_ac, s_v = sem("acv_psum"), sem("a_c_ready"), sem("v_ready")
        s_chain = sem("vector_chain")
        s_var, s_rstd = sem("variance_ready"), sem("rstd_ready")
        s_xt, s_xc = sem("x_transposed_psum"), sem("x_columns_ready")
        s_sim, s_shift, s_exp = sem("sim_psum"), sem("shifted_ready"), sem("exp_ready")
        s_et, s_ec, s_o = sem("exp_transposed_psum"), sem("exp_columns_ready"), sem("attended_psum")
        s_xn = sem("x2_normed_ready")
        s_x2t, s_xhi, s_xlo = sem("x2_transposed_psum"), sem("x2_hi_ready"), sem("x2_lo_ready")
        s_sc, s_diff, s_gap = sem("gate_scores_psum"), sem("score_gap_ready"), sem("gap_tanh_ready")
        s_hot, s_pool_chain = sem("one_hot_ready"), sem("pool_chain")
        s_p16, s_pt, s_pc = sem("probs_ready"), sem("probs_transposed_psum"), sem("prob_columns_ready")
        s_h1, s_h2, s_pb = sem("h1_psum"), sem("h2_psum"), sem("probs_spread_psum")
        s_silu, s_glu, s_hid = sem("silu_ready"), sem("glu_ready"), sem("hidden_ready")
        s_hhi, s_hlo, s_y = sem("hidden_hi_ready"), sem("hidden_lo_ready"), sem("y_added")
        s_last_lo = sem("last_hidden_lo_ready")
        s_w12hi, s_w12lo = sem("w12_hi_ready"), sem("w12_lo_ready")
        s_w3hi, s_w3lo = sem("w3_hi_ready"), sem("w3_lo_ready")
        s_yc, s_yt, s_fin = sem("y_columns_ready"), sem("y_transposed_psum"), sem("result_ready")

        def later(n, at_least):
            return not isinstance(n, int) or n >= at_least

        block = ctx.enter_context(nc.Block())

        @block.sync
        def _(sp):
            sp.dma_start(x_in[:, 0], x_rows[0]).then_inc(s_x[0], 16)
            sp.dma_start(x_in[:, 1], x_rows[1]).then_inc(s_x[1], 16)
            for q in range(4):
                sp.dma_start(w_raw[:, 4 * q:4 * q + 4], weights[:, 4 * q:4 * q + 4]).then_inc(s_w[q], 16)
            sp.wait_ge(s_fin, 1)
            sp.dma_start(out_rows[0], y_out[:, 0]).then_inc(s_out, 16)
            for half, rows in enumerate(HALF_TILES):
                sp.wait_ge(s_fin, 2 + half)
                sp.dma_start(out_rows[1][:, rows], y_out[:, 1, rows]).then_inc(s_out, 16)
            sp.wait_ge(s_out, 16 * 3)

        @block.gpsimd
        def _(pool):
            pool.memset(ident[:], 0.0).then_inc(s_const, 1)
            pool.memset(minus_half[:], -0.5).then_inc(s_const, 1)
            pool.wait_ge(s_const, 2)
            pool.affine_select(out=ident[:], in_=ident[:], compare_op=ALU.not_equal, fill=1.0, base=0,
                               pattern=[[-1, P]], channel_multiplier=1).then_inc(s_const, 1)

            def power(k):
                pool.wait_ge(s_var, k + 1)
                pool.tensor_tensor(out=rstd[:, k], in0=var_eps[:, k], in1=minus_half[:], op=ALU.pow).then_inc(s_rstd, 1)

            power(0)
            power(1)
            pool.memset(ident16[:], 0.0).then_inc(s_const, 1)
            pool.memset(pick[:].rearrange("p e m -> p (e m)").bitcast(F32), 0.0).then_inc(s_const, 1)
            pool.iota(number[:], pattern=[[0, T], [0, 2], [1, E]], base=0, channel_multiplier=0,
                      allow_small_or_imprecise_dtypes=True).then_inc(s_const, 1)
            pool.wait_ge(s_const, 6)
            pool.affine_select(out=ident16[:], in_=ident16[:], compare_op=ALU.not_equal, fill=1.0, base=0,
                               pattern=[[-1, P]], channel_multiplier=1).then_inc(s_const, 1)
            for part in range(3):
                if part:
                    pool.wait_ge(s_const, 7 + part)
                pool.affine_select(out=pick[:], in_=pick[:], compare_op=ALU.not_equal, fill=1.0,
                                   base=-E * part, pattern=[[-1, E], [0, P]], channel_multiplier=1).then_inc(s_const, 1)
            pool.memset(w_raw[:, HALVES:HALVES + AHEAD], 0.0).then_inc(s_const, 1)
            power(2)
            power(3)

            pool_links = [0]

            def pool_chain(*instructions):
                for instruction in instructions:
                    pool_links[0] += 1
                    instruction.then_inc(s_pool_chain, 1)
                pool.wait_ge(s_pool_chain, pool_links[0])

            def probabilities(b):
                pool.wait_ge(s_hot, b + 1)
                pool.wait_ge(s_gap, b + 1)
                pool_chain(*[pool.tensor_scalar(p12[:, b, :, r], half_tanh[:, b], half_gate[:, 1 - r:2 - r],
                                                half_gate[:, 0:1], ALU.mult, ALU.add) for r in range(2)])
                pool_chain(pool.tensor_tensor(out=pr[:, b], in0=hot[:, b],
                                              in1=p12[:, b].unsqueeze(3).broadcast_to([P, T, 2, E]), op=ALU.mult))
                pool_chain(pool.tensor_tensor(out=prob[:, b], in0=pr[:, b, :, 0], in1=pr[:, b, :, 1], op=ALU.add))
                pool_chain(pool.tensor_copy(prob16[:, b, :, 0], prob[:, b]))
                pool_chain(pool.tensor_tensor(out=rest[:, b], in0=prob[:, b], in1=prob16[:, b, :, 0], op=ALU.subtract))
                pool_chain(pool.tensor_copy(prob16[:, b, :, 1], rest[:, b]))
                pool.tensor_tensor(out=prob16[:, b, :, 2], in0=rest[:, b], in1=prob16[:, b, :, 1],
                                   op=ALU.subtract).then_inc(s_p16, 1)

            def low_part(n, k):
                pool.wait_ge(s_hhi, n + 1)
                if later(n, SLOTS):
                    pool.wait_ge(s_y, n - SLOTS + 1)
                pool.tensor_tensor(out=hid_lo[:, k], in0=hid[:, k], in1=hid_hi[:, k],
                                   op=ALU.subtract).then_inc(s_hlo, 1)

            probabilities(0)
            probabilities(1)
            for n in range(PER - 1):
                low_part(n, n % SLOTS)
            with pool.Fori(1, TURNS) as turn:
                for n in range(-1, PER - 1):
                    low_part(turn * PER + n, n % SLOTS)

        @block.scalar
        def _(act):
            act.dma_start(par[:], params).then_inc(s_par, 16)
            act.wait_ge(s_par, 16)
            act.activation(gates[:], par[:, C_GX:C_GX + 2], ACT.Tanh).then_inc(s_gates, 1)

            def x_columns(b):
                act.wait_ge(s_xt, b + 1)
                act.activation(x_col[:, b], ps_x[b][:], ACT.Copy).then_inc(s_xc, 1)

            def exps(b):
                act.wait_ge(s_shift, b + 1)
                act.activation(e_row[:, b], shifted[:, b], ACT.Exp, scale=SCALE).then_inc(s_exp, 1)

            def exp_columns(b):
                act.wait_ge(s_et, b + 1)
                act.activation(e_col[:, b], ps_e[b][0:J, :], ACT.Copy).then_inc(s_ec, 1)

            def x2_high(b):
                act.wait_ge(s_x2t, b + 1)
                act.activation(x2_hi[:, b], ps_x2[b][:], ACT.Copy).then_inc(s_xhi, 1)

            def gap(b):
                act.wait_ge(s_diff, b + 1)
                act.activation(half_tanh[:, b], diff[:, b], ACT.Tanh, scale=0.5).then_inc(s_gap, 1)

            def w12_high(h, k):
                act.activation(w12_hi[:, k], w_raw[:, h, 0:2 * P], ACT.Copy).then_inc(s_w12hi, 1)

            def w3_high(h, k):
                act.activation(w3_hi[:, k], w_raw[:, h, 2 * P:3 * P], ACT.Copy).then_inc(s_w3hi, 1)

            def silu_step(n, k):
                act.wait_ge(s_h1, n + 1)
                if later(n, SLOTS):
                    act.wait_ge(s_glu, n - SLOTS + 1)
                act.activation(silu[:, k], H1[k % 2][:], ACT.Silu).then_inc(s_silu, 1)

            def hidden_high(n, k):
                act.wait_ge(s_hid, n + 1)
                if later(n, SLOTS):
                    act.wait_ge(s_y, n - SLOTS + 1)
                act.activation(hid_hi[:, k], hid[:, k], ACT.Copy).then_inc(s_hhi, 1)

            x_columns(0)
            act.wait_ge(s_kps, 1)
            act.activation(k_col[:], ps_k[:, 0:B * J], ACT.Identity, bias=par[:, C_BK:C_BK + 1]).then_inc(s_k, 1)
            act.wait_ge(s_acv_ps, 1)
            act.activation(a_col[:], ps_a[:, 0:B * J], ACT.Copy).then_inc(s_ac, 1)
            act.wait_ge(s_acv_ps, 2)
            act.activation(c_all[:].rearrange("p b j -> p (b j)"), ps_c[:, 0:B * J], ACT.Copy).then_inc(s_ac, 1)
            x_columns(1)
            act.wait_ge(s_w[0], 16)
            w12_high(0, 0)
            exps(0)
            w12_high(1, 1)
            exps(1)
            exp_columns(0)
            w12_high(2, 2)
            exp_columns(1)
            act.wait_ge(s_const, 2)
            act.activation(table_load[:], minus_half[:], ACT.Silu)
            w12_high(AHEAD, AHEAD)
            for h in range(SLOTS):
                w3_high(h, h)
            x2_high(0)
            for q in range(1, 4):
                act.wait_ge(s_w[q], 16)
            act.wait_ge(s_const, 11)

            def first_turn():
                silu_step(0, 0)
                x2_high(1)
                gap(0)
                silu_step(1, 1)
                silu_step(2, 2)
                gap(1)
                silu_step(3, 3)
                hidden_high(0, 0)
                for n in range(SLOTS, PER):
                    silu_step(n, n % SLOTS)
                    hidden_high(n - 3, (n - 3) % SLOTS)
                    if n >= SLOTS + 1:
                        act.wait_ge(s_h2, n)
                        w12_high(n - 1, n - SLOTS - 1)
                hidden_high(PER - 3, (PER - 3) % SLOTS)
                hidden_high(PER - 2, (PER - 2) % SLOTS)

            def turn_of_steps(n0, h0):
                for n in range(PER):
                    silu_step(n0 + n, n % SLOTS)
                    hidden_high(n0 + n - 1, (n - 1) % SLOTS)
                    if n == 0:
                        act.wait_ge(s_h2, n0)
                        w12_high(h0 + AHEAD, AHEAD)
                    if n < SLOTS:
                        act.wait_ge(s_y, n0 + n - SLOTS + 1)
                        w3_high(h0 + n, n)
                    if n >= SLOTS + 1:
                        act.wait_ge(s_h2, n0 + n)
                        w12_high(h0 + n - 1, n - SLOTS - 1)

            first_turn()
            with act.Fori(1, TURNS) as turn:
                turn_of_steps(turn * PER, turn * (PER // 2))
            act.wait_ge(s_y, STEPS - SLOTS)
            act.activation(y_col[:, 0], Y[0][:], ACT.Copy).then_inc(s_yc, 1)
            act.wait_ge(s_hid, STEPS)
            for cols in HALF_COLS:
                act.activation(hid_hi[:, LAST, cols], hid[:, LAST, cols], ACT.Copy).then_inc(s_hhi, 1)
            act.wait_ge(s_y, STEPS + 1)
            for cols in HALF_COLS:
                act.activation(y_col[:, 1, cols], Y[1][:, cols], ACT.Copy).then_inc(s_yc, 1)

        @block.vector
        def _(dve):
            links = [0]

            def note(instruction):
                links[0] += 1
                instruction.then_inc(s_chain, 1)

            def all_noted():
                dve.wait_ge(s_chain, links[0])

            def chain(instruction):
                note(instruction)
                all_noted()

            dve.memset(zeros_r[:].bitcast(F32), 0.0).then_inc(s_zeros, 1)
            dve.memset(prob_col[:].rearrange("p b n -> p (b n)").bitcast(F32), 0.0).then_inc(s_zeros, 1)

            def part_stats(k, rows):
                for i in range(T):
                    note(dve.bn_stats(stats[:, k, i], rows[:, i]))

            def variances(k):
                all_noted()
                for i in range(T):
                    note(dve.bn_aggr(moments[:, k, i], stats[:, k, i]))
                all_noted()
                dve.tensor_scalar_add(var_eps[:, k], moments[:, k, :, 1], EPS).then_inc(s_var, 1)

            def row_stats(k, rows):
                part_stats(k, rows)
                variances(k)

            def softmax_shift(b):
                dve.wait_ge(s_sim, b + 1)
                dve.wait_ge(s_rstd, b + 1)
                for i in range(T):
                    note(dve.scalar_tensor_tensor(out=sim[:, b, i], in0=tiles(ps_sim[b], J)[:, i],
                                                  scalar=rstd[:, b, i:i + 1], in1=c_all[:, b], op0=ALU.mult, op1=ALU.add))
                all_noted()
                chain(dve.reduce_max(top[:, b], sim[:, b], AX.X))
                dve.tensor_tensor(shifted[:, b], sim[:, b], top[:, b].unsqueeze(2).broadcast_to([P, T, J]),
                                  ALU.subtract).then_inc(s_shift, 1)

            def softmax_scale(b):
                dve.wait_ge(s_exp, b + 1)
                chain(dve.reduce_sum(e_sum[:, b], e_row[:, b], AX.X))
                chain(dve.reciprocal(e_inv[:, b], e_sum[:, b]))
                chain(dve.tensor_scalar(e_scale[:, b], e_inv[:, b], gates[:, 0:1], None, ALU.mult))

            def residual(b):
                dve.wait_ge(s_o, b + 1)
                for i in range(T):
                    note(dve.scalar_tensor_tensor(out=x2[:, b, i], in0=tiles(ps_o[b])[:, i], scalar=e_scale[:, b, i:i + 1],
                                                  in1=x_in[:, b, i], op0=ALU.mult, op1=ALU.add))
                all_noted()

            def normalise(b):
                dve.wait_ge(s_rstd, B + b + 1)
                for i in range(T):
                    dve.tensor_scalar(x2_n[:, b, i], x2[:, b, i], moments[:, B + b, i, 0:1],
                                      rstd[:, B + b, i:i + 1], ALU.subtract, ALU.mult).then_inc(s_xn, 1)

            def x2_low(b):
                dve.wait_ge(s_xhi, b + 1)
                dve.tensor_tensor(x2_lo[:, b], ps_x2[b][:], x2_hi[:, b].bitcast(F32), ALU.subtract).then_inc(s_xlo, 1)

            def best_two(b):
                dve.wait_ge(s_sc, b + 1)
                chain(dve.tensor_copy(sc[:, b], tiles(ps_gate[b], E)))
                for i in range(T):
                    note(dve.max(best[:, b, i], sc[:, b, i]))
                all_noted()
                for i in range(T):
                    note(dve.max_index(which[:, b, i], best[:, b, i], sc[:, b, i]))
                dve.tensor_tensor(diff[:, b], best[:, b, :, 1], best[:, b, :, 0], ALU.subtract).then_inc(s_diff, 1)
                all_noted()
                dve.tensor_tensor(hot[:, b], number[:], which[:, b, :, 0:2].unsqueeze(3).broadcast_to([P, T, 2, E]),
                                  ALU.is_equal).then_inc(s_hot, 1)

            def prob_columns(b):
                dve.wait_ge(s_pt, b + 1)
                dve.tensor_copy(prob_col[0:3 * E, b], ps_prob[b][0:3 * E, 0:TOK // 2].bitcast(BF16)).then_inc(s_pc, 1)

            def w12_low(h, k):
                dve.wait_ge(s_w12hi, h + 1)
                dve.tensor_tensor(w12_lo[:, k], w_raw[:, h, 0:2 * P], w12_hi[:, k].bitcast(F32), ALU.subtract).then_inc(s_w12lo, 1)

            def w3_low(h, k):
                dve.wait_ge(s_w3hi, h + 1)
                dve.tensor_tensor(w3_lo[:, k], w_raw[:, h, 2 * P:3 * P], w3_hi[:, k].bitcast(F32), ALU.subtract).then_inc(s_w3lo, 1)

            dve.wait_ge(s_x[0], 16)
            row_stats(0, x_in[:, 0])
            dve.wait_ge(s_par, 16)
            chain(dve.bn_stats(wq_stats[:], par[:, C_WQT:C_WQT + D]))
            chain(dve.bn_aggr(wq_mean[:], wq_stats[:]))
            dve.tensor_scalar(wq_centred[:], par[:, C_WQT:C_WQT + D], wq_mean[:, 0:1], None, ALU.subtract).then_inc(s_wq, 1)
            dve.wait_ge(s_x[1], 16)
            row_stats(1, x_in[:, 1])
            note(dve.tensor_copy(gate_hi[:], par[:, C_GATE:C_GATE + E]))
            dve.wait_ge(s_gates, 1)
            note(dve.tensor_scalar(half_gate[:, 0:1], gates[:, 1:2], 0.5, None, ALU.mult))
            note(dve.tensor_scalar(half_gate[:, 1:2], gates[:, 1:2], -0.5, None, ALU.mult))
            all_noted()
            note(dve.tensor_tensor(gate_lo[:], par[:, C_GATE:C_GATE + E], gate_hi[:].bitcast(F32), ALU.subtract))
            dve.wait_ge(s_ac, 2)
            softmax_shift(0)
            dve.wait_ge(s_acv_ps, 3)
            for b in range(B):
                last = dve.tensor_tensor(v_row[:, b], ps_v[0:J, b * D:(b + 1) * D], par[0:J, C_BV:C_BV + D], ALU.add)
            last.then_inc(s_v, 1)
            softmax_shift(1)
            softmax_scale(0)
            softmax_scale(1)
            w12_low(0, 0)
            residual(0)
            row_stats(B, x2[:, 0])
            residual(1)
            normalise(0)
            part_stats(B + 1, x2[:, 1])
            x2_low(0)
            variances(B + 1)
            w12_low(1, 1)
            normalise(1)
            dve.wait_ge(s_const, 6)
            best_two(0)

            def glu_step(n, k):
                dve.wait_ge(s_silu, n + 1)
                dve.wait_ge(s_h2, n + 1)
                dve.tensor_tensor(glu[:, k], silu[:, k], H2[k % 2][:], ALU.mult).then_inc(s_glu, 1)

            def hidden_step(n, k, s):
                dve.wait_ge(s_glu, n + 1)
                dve.wait_ge(s_pb, s + 1)
                if later(n, SLOTS):
                    dve.wait_ge(s_hlo, n - SLOTS + 1)
                dve.tensor_tensor(hid[:, k], glu[:, k], PB[k // 2][:], ALU.mult).then_inc(s_hid, 1)

            def first_turn():
                x2_low(1)
                w12_low(2, 2)
                for n in range(PER + 1):
                    if n < PER:
                        glu_step(n, n % SLOTS)
                    if n == 1:
                        w12_low(AHEAD, AHEAD)
                        w3_low(0, 0)
                        best_two(1)
                        for h in range(1, SLOTS):
                            w3_low(h, h)
                        prob_columns(0)
                    if n >= 2:
                        hidden_step(n - 2, (n - 2) % SLOTS, (n - 2) // 2)
                    if n == 4:
                        prob_columns(1)
                    if SLOTS + 1 <= n < PER:
                        w12_low(n - 1, n - SLOTS - 1)
                hidden_step(PER - 1, (PER - 1) % SLOTS, (PER - 1) // 2)

            def turn_of_steps(n0, h0):
                for n in range(PER):
                    glu_step(n0 + n, n % SLOTS)
                    hidden_step(n0 + n, n % SLOTS, h0 + n // 2)
                    if n == 0:
                        w12_low(h0 + AHEAD, AHEAD)
                    if n < SLOTS:
                        w3_low(h0 + n, n)
                    if n >= SLOTS + 1:
                        w12_low(h0 + n - 1, n - SLOTS - 1)

            first_turn()
            with dve.Fori(1, TURNS) as turn:
                turn_of_steps(turn * PER, turn * (PER // 2))
            for half, cols in enumerate(HALF_COLS):
                dve.wait_ge(s_hhi, STEPS + half)
                if half == 0:
                    dve.wait_ge(s_y, STEPS - SLOTS)
                dve.tensor_tensor(hid_lo[:, LAST, cols], hid[:, LAST, cols], hid_hi[:, LAST, cols].bitcast(F32),
                                  ALU.subtract).then_inc(s_last_lo, 1)
            dve.wait_ge(s_yt, 1)
            dve.tensor_tensor(y_out[:, 0], x2[:, 0], tiles(ps_fin[0]), ALU.add).then_inc(s_fin, 1)
            for half, rows in enumerate(HALF_TILES):
                dve.wait_ge(s_yt, 2 + half)
                dve.tensor_tensor(y_out[:, 1, rows], x2[:, 1, rows], tiles(ps_fin[1 + half])[:, rows],
                                  ALU.add).then_inc(s_fin, 1)

        @block.tensor
        def _(pe):
            def x_transposes(b):
                pe.wait_ge(s_x[b], 16)
                for i in range(T):
                    last = pe.transpose(tiles(ps_x[b])[:, i], x_in[:, b, i], ident[:])
                last.then_inc(s_xt, 1)

            def scores(b):
                pe.wait_ge(s_xc, b + 1)
                for i in range(T):
                    last = pe.matmul(tiles(ps_sim[b], J)[:, i], x_col[:, b, i * P:(i + 1) * P],
                                     a_col[:, b * J:(b + 1) * J], start=True, stop=True)
                last.then_inc(s_sim, 1)

            def exp_transposes(b):
                pe.wait_ge(s_exp, b + 1)
                for i in range(T):
                    last = pe.transpose(tiles(ps_e[b])[0:J, i], e_row[:, b, i], ident[:])
                last.then_inc(s_et, 1)

            def attend(b):
                pe.wait_ge(s_ec, b + 1)
                for i in range(T):
                    last = pe.matmul(tiles(ps_o[b])[:, i], e_col[:, b, i * P:(i + 1) * P], v_row[:, b], start=True, stop=True)
                last.then_inc(s_o, 1)

            def x2_transposes(b):
                for i in range(T):
                    pe.wait_ge(s_xn, b * T + i + 1)
                    last = pe.transpose(tiles(ps_x2[b])[:, i], x2_n[:, b, i], ident[:])
                last.then_inc(s_x2t, 1)

            def gate_scores(b):
                pe.wait_ge(s_xlo, b + 1)
                for i in range(T):
                    gate = tiles(ps_gate[b], E)[:, i]
                    cols = slice(i * P, (i + 1) * P)
                    pe.matmul(gate, x2_hi[:, b, cols], gate_hi[:], start=True, stop=False)
                    pe.matmul(gate, x2_hi[:, b, cols], gate_lo[:], start=False, stop=False)
                    last = pe.matmul(gate, x2_lo[:, b, cols], gate_hi[:], start=False, stop=True)
                last.then_inc(s_sc, 1)

            def prob_transposes(b):
                pe.wait_ge(s_p16, b + 1)
                for i in range(T):
                    last = pe.transpose(ps_prob[b][0:3 * E, i * P // 2:(i + 1) * P // 2].bitcast(BF16),
                                        prob16[:, b, i].rearrange("p a e -> p (a e)"), ident16[:])
                last.then_inc(s_pt, 1)

            def y_zero(b):
                pe.wait_ge(s_pc, b + 1)
                pe.matmul(Y[b][:], zeros_r[:, 0:P], zeros_r[:], start=True, stop=False, skip_group_check=True)

            def keep_warm(passes):
                for _ in range(passes):
                    pe.matmul(H1[1][:], zeros_r[:, 0:P], zeros_r[:], start=True, stop=True)

            pe.wait_ge(s_zeros, 1)
            keep_warm(4)
            pe.wait_ge(s_const, 3)
            x_transposes(0)
            pe.wait_ge(s_par, 16)
            ctx_col = par[:, C_CTX:C_CTX + B * J]
            pe.matmul(ps_k[:, 0:B * J], par[:, C_WK:C_WK + D], ctx_col, start=True, stop=True).then_inc(s_kps, 1)
            keep_warm(1)
            pe.wait_ge(s_k, 1)
            pe.wait_ge(s_wq, 1)
            pe.matmul(ps_a[:, 0:B * J], wq_centred[:], k_col[:], start=True, stop=True).then_inc(s_acv_ps, 1)
            pe.matmul(ps_c[:, 0:B * J], par[:, C_BQ:C_BQ + 1].broadcast_to([P, P]), k_col[:],
                      start=True, stop=True).then_inc(s_acv_ps, 1)
            x_transposes(1)
            pe.wait_ge(s_ac, 1)
            scores(0)
            for b in range(B):
                last = pe.matmul(ps_v[0:J, b * D:(b + 1) * D], ctx_col[:, b * J:(b + 1) * J], par[:, C_WV:C_WV + D],
                                 start=True, stop=True)
            last.then_inc(s_acv_ps, 1)
            scores(1)
            keep_warm(7)
            pe.wait_ge(s_ac, 2)
            pe.wait_ge(s_v, 1)
            exp_transposes(0)
            keep_warm(4)
            exp_transposes(1)
            attend(0)
            attend(1)

            def up(n, h, k, b):
                if b == 0:
                    pe.wait_ge(s_w12lo, h + 1)
                if later(n, 2):
                    pe.wait_ge(s_glu, n - 1)
                for part, (bank_, ready) in enumerate(((H1[k % 2], s_h1), (H2[k % 2], s_h2))):
                    cols = slice(part * P, (part + 1) * P)
                    pe.matmul(bank_[:], w12_hi[:, k, cols], x2_hi[:, b], start=True, stop=False)
                    pe.matmul(bank_[:], w12_hi[:, k, cols], x2_lo[:, b], start=False, stop=False)
                    pe.matmul(bank_[:], w12_lo[:, k, cols], x2_hi[:, b], start=False, stop=True).then_inc(ready, 1)

            def spread(n, e, s, b):
                if later(n, SLOTS):
                    pe.wait_ge(s_hid, n - 2)
                pe.matmul(PB[s][:], pick[:, e], prob_col[:, b], start=True, stop=True).then_inc(s_pb, 1)

            def down(n, h, k, b):
                pe.wait_ge(s_hlo, n + 1)
                if b == 0:
                    pe.wait_ge(s_w3lo, h + 1)
                pe.matmul(Y[b][:], w3_hi[:, k], hid_hi[:, k], start=False, stop=False, skip_group_check=True)
                pe.matmul(Y[b][:], w3_hi[:, k], hid_lo[:, k], start=False, stop=False, skip_group_check=True)
                pe.matmul(Y[b][:], w3_lo[:, k], hid_hi[:, k], start=False, stop=True,
                          skip_group_check=True).then_inc(s_y, 1)

            def first_turn():
                pe.wait_ge(s_w12lo, 1)
                pe.wait_ge(s_xhi, 1)
                for part, bank_ in enumerate((H1[0], H2[0])):
                    cols = slice(part * P, (part + 1) * P)
                    pe.matmul(bank_[:], w12_hi[:, 0, cols], x2_hi[:, 0], start=True, stop=False)
                    pe.matmul(bank_[:], w12_lo[:, 0, cols], x2_hi[:, 0], start=False, stop=False)
                gate_scores(0)
                for part, (bank_, ready) in enumerate(((H1[0], s_h1), (H2[0], s_h2))):
                    pe.matmul(bank_[:], w12_hi[:, 0, part * P:(part + 1) * P], x2_lo[:, 0],
                              start=False, stop=True).then_inc(ready, 1)
                x2_transposes(1)
                up(1, 1, 1, 0)
                gate_scores(1)
                up(2, 2, 2, 0)
                prob_transposes(0)
                up(3, 3, 3, 0)
                y_zero(0)
                spread(0, 0, 0, 0)
                spread(2, 1, 1, 0)
                up(4, 0, 0, 1)
                prob_transposes(1)
                up(5, 1, 1, 1)
                down(0, 0, 0, 0)
                up(6, 2, 2, 1)
                down(1, 1, 1, 0)
                y_zero(1)
                spread(4, 0, 0, 1)
                up(7, 3, 3, 1)
                down(2, 2, 2, 0)
                spread(6, 1, 1, 1)
                down(3, 3, 3, 0)
                down(4, 0, 0, 1)

            def turn_of_steps(n0, h0, e0):
                for n in range(PER):
                    up(n0 + n, h0 + n % SLOTS, n % SLOTS, n // SLOTS)
                    if n % 2 == 0:
                        spread(n0 + n, e0 + n // 2 % 2, n // 2 % 2, n // SLOTS)
                    m = (n - LAG) % PER
                    down(n0 + (n - LAG), h0 + m % SLOTS, m % SLOTS, m // SLOTS)

            pe.wait_ge(s_zeros, 2)
            keep_warm(14)
            x2_transposes(0)
            keep_warm(3)
            pe.wait_ge(s_const, 10)
            first_turn()
            with pe.Fori(1, TURNS) as turn:
                turn_of_steps(turn * PER, turn * (PER // 2), turn * (PER // 4))

            def y_transposes(k, b, rows):
                pe.wait_ge(s_yc, k + 1)
                for i in range(rows.start, rows.stop):
                    last = pe.transpose(tiles(ps_fin[k])[:, i], y_col[:, b, i * P:(i + 1) * P], ident[:])
                last.then_inc(s_yt, 1)

            for n in range(STEPS - LAG, STEPS - 1):
                down(n, HALVES - STEPS + n, n % SLOTS, 1)
                if n == STEPS - LAG:
                    pe.wait_ge(s_glu, STEPS - 1)
                    y_transposes(0, 0, slice(0, T))
            for half, cols in enumerate(HALF_COLS):
                pe.wait_ge(s_last_lo, half + 1)
                pe.wait_ge(s_w3lo, HALVES)
                for w3, hidden in ((w3_hi, hid_hi), (w3_hi, hid_lo)):
                    pe.matmul(Y[1][:, cols], w3[:, LAST], hidden[:, LAST, cols], start=False, stop=False,
                              skip_group_check=True)
                pe.matmul(Y[1][:, cols], w3_lo[:, LAST], hid_hi[:, LAST, cols], start=False, stop=True,
                          skip_group_check=True).then_inc(s_y, 1)
            for half, rows in enumerate(HALF_TILES):
                y_transposes(1 + half, 1, rows)


def kernel(x, ctx_1024, g_xattn, g_ffn, L0_xattn_Wq, L0_xattn_bq, L0_xattn_Wk, L0_xattn_bk, L0_xattn_Wv,
           L0_xattn_bv, L0_ffn_w12, L0_ffn_w3, L0_ffn_gate_w):
    import numpy as np
    import concourse.bacc as bacc
    from concourse.bass_utils import run_bass_kernel_spmd

    columns = [
        np.transpose(L0_xattn_Wq), L0_xattn_Wk, L0_xattn_Wv, np.transpose(L0_ffn_gate_w),
        np.reshape(L0_xattn_bq, (D, 1)), np.reshape(L0_xattn_bk, (D, 1)),
        np.broadcast_to(np.reshape(g_xattn, (1, 1)), (D, 1)), np.broadcast_to(np.reshape(g_ffn, (1, 1)), (D, 1)),
        np.broadcast_to(np.reshape(L0_xattn_bv, (1, D)), (D, D)),
        np.reshape(np.transpose(ctx_1024, (2, 0, 1)), (D, B * J)),
    ]
    w12 = np.reshape(L0_ffn_w12, (E, 2, 2, P, D))
    w12 = np.transpose(w12, (4, 0, 2, 1, 3))
    w3 = np.transpose(np.reshape(L0_ffn_w3, (E, D, 2, P)), (3, 0, 2, 1))
    weights = np.concatenate([np.reshape(w12, (P, HALVES, 2 * P)), np.reshape(w3, (P, HALVES, P))], axis=2)
    arrays = {
        "x": np.ascontiguousarray(x),
        "params": np.ascontiguousarray(np.concatenate(columns, axis=1)),
        "weights": np.ascontiguousarray(weights),
    }
    nc = bacc.Bacc("TRN2", target_bir_lowering=False, num_devices=1)
    aps = [nc.dram_tensor(name, a.shape, mybir.dt.from_np(a.dtype), kind="ExternalInput").ap()
           for name, a in arrays.items()]
    out = nc.dram_tensor("out", (B, TOK, D), F32, kind="ExternalOutput").ap()
    build(nc, *aps, out)
    result = run_bass_kernel_spmd(nc, [arrays], core_ids=[0])
    return result.results[0]["out"]
```
